# Optimizing a Trainium2 kernel written in Bass

```python
import numpy as np
import jax
import jax.numpy as jnp

def _softmax(x, axis=-1):
    return jax.nn.softmax(x, axis=axis)

def _gelu(x):
    return jax.nn.gelu(x, approximate=True)

def _silu(x):
    return jax.nn.silu(x)

def _sigmoid(x):
    return jax.nn.sigmoid(x)

def _layernorm(x, axis=-1, eps=1e-05):
    m = jnp.mean(x, axis=axis, keepdims=True)
    v = jnp.var(x, axis=axis, keepdims=True)
    return (x - m) / jnp.sqrt(v + eps)

def _scatter_add(tgt, idx, src, axis=0):
    return tgt.at[idx].add(src)

def _segment_sum(src, seg, n):
    return jax.ops.segment_sum(src, seg, n)
kernel_name = 'mk_gnn_resnorm_d1_gnn_r32_cc0365'

def setup_inputs(seed: int=0):
    np.random.seed(seed)
    _w = jnp.asarray

    def _rec_inputs():
        import jax
        import jax.numpy as jnp
        _gk = jax.random.key(seed)
        x = -0.0004402 + 1 * jax.random.normal(jax.random.fold_in(_gk, 1), (3125, 16), jnp.float32)
        src = jax.random.randint(jax.random.fold_in(_gk, 2), (100000,), 0, 3125, jnp.int32)
        dst = jax.random.randint(jax.random.fold_in(_gk, 3), (100000,), 0, 3125, jnp.int32)
        _o = jnp.argsort(dst, stable=True)
        src = src[_o]
        dst = dst[_o]
        edge_attr_16 = -3.57403e-05 + 0.999761 * jax.random.normal(jax.random.fold_in(_gk, 12), (100000, 16), jnp.float32)
        return (x, src, dst, edge_attr_16)
    x, src, dst, edge_attr_16 = _rec_inputs()

    def _L0_gnn_setup():
        import jax, jax.numpy as jnp
        import numpy as np
        N_NODES = 30000
        N_EDGES = 9375
        IN_FEATS = 16
        OUT_FEATS = 16
        EDGE_DIM = 16
        key = jax.random.key(seed)
        ks = jax.random.split(key, 8)
        feat = jax.random.normal(ks[0], (N_NODES, IN_FEATS), dtype=jnp.float32)
        efeat = jax.random.normal(ks[1], (N_EDGES, EDGE_DIM), dtype=jnp.float32)
        W_msg = jax.random.normal(ks[2], (EDGE_DIM, IN_FEATS * OUT_FEATS), dtype=jnp.float32) * 0.1
        b_msg = jnp.zeros((IN_FEATS * OUT_FEATS,), dtype=jnp.float32)
        W_attn = jax.random.normal(ks[3], (EDGE_DIM, IN_FEATS * OUT_FEATS), dtype=jnp.float32) * 0.1
        b_attn = jnp.zeros((IN_FEATS * OUT_FEATS,), dtype=jnp.float32)
        src = jax.random.randint(ks[4], (N_EDGES,), 0, N_NODES, dtype=jnp.int32)
        dst = jax.random.randint(ks[5], (N_EDGES,), 0, N_NODES, dtype=jnp.int32)
        return {'feat': feat, 'efeat': efeat, 'W_msg': W_msg, 'b_msg': b_msg, 'W_attn': W_attn, 'b_attn': b_attn, 'src': src, 'dst': dst}
    _L0_gnn_all = _L0_gnn_setup()
    _L0_gnn_in = {k: v for k, v in _L0_gnn_all.items() if k in ('W_msg', 'b_msg', 'W_attn', 'b_attn')}
    del _L0_gnn_all
    return {'x': x, 'src': src, 'dst': dst, 'edge_attr_16': edge_attr_16, 'L0_gnn_W_msg': _L0_gnn_in['W_msg'], 'L0_gnn_b_msg': _L0_gnn_in['b_msg'], 'L0_gnn_W_attn': _L0_gnn_in['W_attn'], 'L0_gnn_b_attn': _L0_gnn_in['b_attn']}

def reference(x, src, dst, edge_attr_16, L0_gnn_W_msg, L0_gnn_b_msg, L0_gnn_W_attn, L0_gnn_b_attn):
    import jax
    import jax.numpy as jnp

    def _L0_gnn_ref(feat, efeat, W_msg, b_msg, W_attn, b_attn, src, dst):
        import jax, jax.numpy as jnp
        import numpy as np
        N_NODES = 30000
        N_EDGES = 9375
        IN_FEATS = 16
        OUT_FEATS = 16
        EDGE_DIM = 16
        N, in_f = feat.shape
        E = efeat.shape[0]
        w_m = (efeat @ W_msg + b_msg).reshape(E, in_f, -1)
        w_a = (efeat @ W_attn + b_attn).reshape(E, in_f, -1)
        h_src = feat[src][:, :, None]
        e1 = w_m * h_src
        e2 = w_a * h_src
        seg_max = jax.ops.segment_max(e2, dst, num_segments=N)
        ex = jnp.exp(e2 - seg_max[dst])
        denom = jax.ops.segment_sum(ex, dst, num_segments=N)
        attn = ex / denom[dst]
        ft = jax.ops.segment_sum(e1 * attn, dst, num_segments=N)
        return ft.sum(axis=1)
    x = _layernorm(x + _L0_gnn_ref(x, edge_attr_16, L0_gnn_W_msg, L0_gnn_b_msg, L0_gnn_W_attn, L0_gnn_b_attn, src, dst), axis=-1)
    return x

_drawn_inputs = setup_inputs


def setup_inputs(seed=0):
    import zlib

    import numpy as np

    out = dict(_drawn_inputs(seed))
    spreads = {'L0_gnn_b_msg': (0.0, 0.1), 'L0_gnn_b_attn': (0.0, 0.1)}
    factors = {}
    for name, (base, spread) in spreads.items():
        noise = np.random.default_rng([zlib.crc32(name.encode()), seed]).standard_normal(out[name].shape)
        drawn = base * np.exp(spread * noise) if base else spread * noise
        out[name] = jnp.asarray(drawn.astype(out[name].dtype))
    for name, factor in factors.items():
        out[name] = (out[name] * factor).astype(out[name].dtype)
    return out
```

```python
from contextlib import ExitStack

import concourse.bass as bass
from concourse import mybir

F32 = mybir.dt.float32
BF16 = mybir.dt.bfloat16
I32 = mybir.dt.int32
ALU = mybir.AluOpType
ACT = mybir.ActivationFunctionType
AX = mybir.AxisListType

P = 128
NUM_NODES = 3125
NUM_EDGES = 100000
FEAT = 16
SLOTS = 8
NUM_BLOCKS = NUM_EDGES // SLOTS
REC = SLOTS * FEAT + 2 * SLOTS
NODE_COLS = 25
NUM_ROWS = P * NODE_COLS
SEG = NUM_EDGES // 125
SUB = SEG // SLOTS
TILES = 4 * -(-(NUM_BLOCKS + NUM_ROWS) // (4 * P))
CHUNKS = TILES * P
RECORDS = 2 * TILES
ATT = FEAT * FEAT
BOTH = 2 * ATT
KROWS = 6 * FEAT + 4
NEG = -2.0 ** 99
CUT = -2.0 ** 101
SKIP = 60000.0
EPS = 1e-5
RING = 4


def gnn_kernel(nc, rec_d, dst_d, sub_last_d, seg_last_d, x_d, w_d, b_d, out_d):
    xpad_d = nc.dram_tensor("xpad", [NUM_NODES + 1, FEAT], F32, kind="Internal").ap()
    chunk_d = nc.dram_tensor("chunk_table", [CHUNKS, 2], F32, kind="Internal").ap()
    mask_d = nc.dram_tensor("mask_table", [TILES, 2 * ATT], BF16, kind="Internal").ap()
    recnode_d = nc.dram_tensor("record_nodes", [RECORDS], F32, kind="Internal").ap()
    recidx_d = nc.dram_tensor("record_index", [RECORDS], I32, kind="Internal").ap()
    sums_d = nc.dram_tensor("sums", [NUM_ROWS + RECORDS, BOTH], F32, kind="Internal").ap()

    with ExitStack() as ctx:
        def sb(name, shape, dt=F32):
            return ctx.enter_context(nc.sbuf_tensor(name, shape, dt))

        def ps(name, shape, dt=F32):
            return ctx.enter_context(nc.psum_tensor(name, shape, dt))

        def sem(name):
            return ctx.enter_context(nc.semaphore(name))

        row_iota = sb("row_iota", [P, P])
        part_iota = sb("part_iota", [P, 1])
        node_iota = sb("node_iota", [P, NODE_COLS + 1])
        chunk_iota = sb("chunk_iota", [TILES, P])
        twice_tile = sb("twice_tile", [TILES, 1])
        ident = sb("ident", [P, P])
        ident16 = sb("ident16", [P, P], BF16)
        before = sb("before", [P, P])
        zeros = sb("zeros", [P, BOTH])
        ones = sb("ones", [1, FEAT])
        w_all = sb("w_all", [17, BOTH])
        w_rest = sb("w_rest", [17, BOTH])
        w_part = sb("w_part", [17, 3, BOTH], BF16)
        w_neg = sb("w_neg", [1, BOTH], BF16)
        w_rows = sb("w_rows", [KROWS, BOTH], BF16)
        seg_last = sb("seg_last", [P, 125], I32)
        sub_last = sb("sub_last", [P, NODE_COLS + 1, SUB], I32)
        blk_dst = sb("blk_dst", [P, NODE_COLS + 1, SLOTS], I32)
        less = sb("less", [P, NODE_COLS + 1, 125])
        seg_f = sb("seg_f", [P, NODE_COLS + 1])
        seg_i = sb("seg_i", [P, NODE_COLS + 1], I32)
        blk_f = sb("blk_f", [P, NODE_COLS + 1])
        blk_i = sb("blk_i", [P, NODE_COLS + 1], I32)
        start = sb("start", [P, NODE_COLS + 1])
        start_i = sb("start_i", [P, NODE_COLS + 1], I32)
        last_i = sb("last_i", [P, NODE_COLS + 1], I32)
        blk0 = sb("blk0", [P, NODE_COLS + 1])
        blk1 = sb("blk1", [P, NODE_COLS + 1])
        tmp = sb("tmp", [P, NODE_COLS + 1])
        num_chunks = sb("num_chunks", [P, NODE_COLS])
        chunk_sum = sb("chunk_sum", [P, NODE_COLS])
        carry = sb("carry", [P, 1])
        chunk0_i = sb("chunk0_i", [P, NODE_COLS], I32)
        entry = sb("entry", [P, NODE_COLS, 2])
        has_edges = sb("has_edges", [P, NODE_COLS])
        table = sb("table", [TILES, P, 2])
        filled = sb("filled", [TILES, 2, P])
        tile_last = sb("tile_last", [2, TILES + 1])
        tile_carry = sb("tile_carry", [TILES, 2])
        c_node = sb("c_node", [TILES, P])
        c_blk = sb("c_blk", [TILES, P])
        c_row = sb("c_row", [TILES, P])
        c_idx = sb("c_idx", [TILES, P])
        c_a = sb("c_a", [TILES, P])
        c_b = sb("c_b", [TILES, P])
        c_ends = sb("c_ends", [TILES, 2])
        c_ext = sb("c_ext", [TILES, 1])
        c_mask = sb("c_mask", [TILES, 2, 2, P], BF16)
        t_node = sb("t_node", [P, TILES])
        t_blk = sb("t_blk", [P, TILES])
        t_row = sb("t_row", [P, TILES])
        t_idx = sb("t_idx", [P, TILES])
        blk_idx = sb("blk_idx", [P, RING], I32)
        rec = sb("rec", [P, RING, REC])
        src1 = sb("src1", [P, 2, SLOTS])
        x_idx = sb("x_idx", [P, RING, SLOTS], I32)
        h = sb("h", [P, RING, SLOTS * FEAT])
        rest = sb("rest", [P, 2, SLOTS, FEAT])
        parts = sb("parts", [P, 2, SLOTS, KROWS], BF16)
        partsT = sb("partsT", [KROWS, 2, SLOTS * P], BF16)
        em = sb("em", [P, RING, SLOTS, FEAT, 2, FEAT])
        max4 = sb("max4", [P, 4, FEAT, FEAT])
        max2 = sb("max2", [P, 2, FEAT, FEAT])
        chunk_max = sb("chunk_max", [P, 2, ATT])
        mask = sb("mask", [P, 2, 2, ATT], BF16)
        fwd_max = sb("fwd_max", [P, ATT])
        node_max = sb("node_max", [P, 2, ATT])
        row_onehot = sb("row_onehot", [P, RING, P])
        sum_rows = sb("sum_rows", [P, RING, BOTH])
        sum_idx = sb("sum_idx", [P, RING], I32)
        rec_max = sb("rec_max", [P, 2, TILES, 2])
        rec_node = sb("rec_node", [P, RECORDS])
        rec_idx = sb("rec_idx", [P, 2], I32)
        rec_idxrow = sb("rec_idxrow", [1, RECORDS], I32)
        r_shift = sb("r_shift", [P, 2, RECORDS])
        r_weight = sb("r_weight", [P, 2, RECORDS])
        r_masks = sb("r_masks", [P, 3, RECORDS])
        r_sum = sb("r_sum", [P, 4, RECORDS])
        r_acc = sb("r_acc", [P, 4, RECORDS])
        x_rows = sb("x_rows", [P, NODE_COLS * FEAT])
        out_rows = sb("out_rows", [P, NODE_COLS * FEAT])
        f_sum = sb("f_sum", [P, NODE_COLS, FEAT])
        f_mid = sb("f_mid", [P, NODE_COLS, FEAT])
        f_stat = sb("f_stat", [P, 4, NODE_COLS])
        eps = sb("eps", [P, 1])

        bank_prod = [ps(f"bank_prod{i}", [P, 2, BOTH]) for i in range(2)]
        bank_t = ps("bank_t", [P, SLOTS * P], BF16)
        bank_max = ps("bank_max", [P, BOTH])
        bank_maxT = ps("bank_maxT", [P, BOTH])
        bank_sum = ps("bank_sum", [P, BOTH])
        maxT_ps = bank_maxT[:, 0:ATT]
        max_ps = bank_max[:, 0:ATT]

        iotas = sem("iotas")
        dve = sem("dve_step")
        loads = sem("loads")
        xpad_done = sem("xpad_done")
        zeroed = sem("zeroed")
        seg_ready = sem("seg_ready")
        sub_landed = sem("sub_landed")
        blk_ready = sem("blk_ready")
        dst_landed = sem("dst_landed")
        consts = sem("consts")
        total_ready = sem("total_ready")
        carry_ps = sem("carry_ps")
        entry_ready = sem("entry_ready")
        entry_stored = sem("entry_stored")
        table_landed = sem("table_landed")
        last_ready = sem("last_ready")
        last_ps = sem("last_ps")
        chunk_ready = sem("chunk_ready")
        chunk_ps = sem("chunk_ps")
        chunk_cols = sem("chunk_cols")
        masks_stored = sem("masks_stored")
        recnode_landed = sem("recnode_landed")
        recidx_ready = sem("recidx_ready")
        recidx_landed = sem("recidx_landed")
        w_split = sem("w_split")
        w_placed = sem("w_placed")

        blk_idx_ready = sem("blk_idx_ready")
        rec_landed = [sem(f"rec_landed{u}") for u in range(RING)]
        src_step = sem("src_step")
        x_idx_ready = sem("x_idx_ready")
        h_landed = [sem(f"h_landed{u}") for u in range(RING)]
        inv_ready = sem("inv_ready")
        part1 = sem("part1")
        rest1 = sem("rest1")
        part2 = sem("part2")
        rest2 = sem("rest2")
        part3 = sem("part3")
        t_ready = sem("t_ready")
        t_copied = sem("t_copied")
        prod_ready = sem("prod_ready")
        times_h = sem("times_h")
        max_step = sem("max_step")
        maxT_ready = sem("maxT_ready")
        fwd_done = sem("fwd_done")
        rev_done = sem("rev_done")
        max_back = sem("max_back")
        shifted = sem("shifted")
        exp_done = sem("exp_done")
        weighted = sem("weighted")
        onehot_ready = sem("onehot_ready")
        sums_ready = sem("sums_ready")
        sums_copied = sem("sums_copied")
        sum_idx_ready = sem("sum_idx_ready")
        rows_stored = [sem(f"rows_stored{u}") for u in range(RING)]
        mask_landed = [sem(f"mask_landed{u}") for u in range(2)]
        rec_max_ready = sem("rec_max_ready")

        r_loaded = sem("r_loaded")
        pool_go = sem("pool_go")
        r_grouped = sem("r_grouped")
        r_t = sem("r_t")
        r_diff = sem("r_diff")
        r_exp = sem("r_exp")
        r_total = sem("r_total")
        r_back = sem("r_back")
        r_rows = sem("r_rows")
        r_stored = sem("r_stored")
        f_loaded = [sem(f"f_loaded{u}") for u in range(2)]
        f_used = sem("f_used")
        x_landed = sem("x_landed")
        f_var = sem("f_var")
        f_std = sem("f_std")
        f_out = sem("f_out")
        out_stored = sem("out_stored")

        block = ctx.enter_context(nc.Block())

        def bc(ap, axis, shape):
            return ap.unsqueeze(axis).to_broadcast(shape)

        FIRST, LAST = -3, TILES + 2
        STEADY = (8, TILES - 4)

        def steps(eng, body):
            for t in range(FIRST - 1, STEADY[0]):
                body(t, t % RING)
            with eng.Fori(STEADY[0], STEADY[1] - RING + 1, RING) as t0:
                for u in range(RING):
                    body(t0 + u, u)
            for t in range(STEADY[1], LAST + 1):
                body(t, t % RING)

        def valid(t, shift):
            return not isinstance(t, int) or 0 <= t + shift < TILES

        def since(eng, s, count):
            if not isinstance(count, int) or count > 0:
                eng.wait_ge(s, count)

        def landed(eng, ring, t, u, each=1, size=RING):
            if isinstance(t, int):
                since(eng, ring[u], 16 * each * (t // size + 1))
            else:
                eng.wait_ge(ring[u], (t - u) * (16 * each // size) + 16 * each)

        @block.sync
        def _(sp):
            sp.dma_start(seg_last[:, :], seg_last_d.partition_broadcast(P)).then_inc(loads, 16)
            sp.dma_start(w_all[0:16, :], w_d).then_inc(loads, 16)
            sp.dma_start(w_all[16:17, :], b_d).then_inc(loads, 16)
            sp.dma_start(xpad_d[1:NUM_NODES + 1, :], x_d).then_inc(xpad_done, 16)
            sp.wait_ge(consts, 2)
            sp.dma_start(xpad_d[0:1, :], ones[:, :]).then_inc(xpad_done, 16)
            sp.dma_start(chunk_d.rearrange("(t j) c -> t (j c)", t=TILES), zeros[0:TILES, 0:2 * P]).then_inc(zeroed, 16)
            for a in range(2):
                sp.dma_start(sums_d[NUM_ROWS + a * TILES:NUM_ROWS + (a + 1) * TILES, :],
                             zeros[0:TILES, :]).then_inc(zeroed, 16)
            sp.wait_ge(w_split, 1)
            for k, part in enumerate([0, 1, 2, 0, 1, 0]):
                sp.dma_start(w_rows[16 * k:16 * k + 16, :], w_part[0:16, part, :]).then_inc(w_placed, 16)
            for part in range(3):
                sp.dma_start(w_rows[96 + part:97 + part, :], w_part[16:17, part, :]).then_inc(w_placed, 16)
            sp.dma_start(w_rows[99:100, :], w_neg[:, :]).then_inc(w_placed, 16)
            sp.wait_ge(entry_stored, 16 * NODE_COLS)
            sp.dma_start(table[:, :, :], chunk_d.rearrange("(t j) c -> t j c", t=TILES)).then_inc(table_landed, 16)
            sp.wait_ge(chunk_ready, 1)
            sp.dma_start(mask_d, c_mask[:, :, :, :].rearrange("t a b j -> t (a b j)")).then_inc(masks_stored, 16)
            sp.dma_start(recnode_d.rearrange("(t a) -> t a", a=2), c_ends[:, :]).then_inc(masks_stored, 16)
            sp.wait_ge(masks_stored, 32)
            sp.dma_start(rec_node[:, :], recnode_d.partition_broadcast(P)).then_inc(recnode_landed, 16)

            def step(t, u):
                if valid(t, 2):
                    since(sp, rev_done, t + 1)
                    v = (u + 2) % 2
                    row = t + 2
                    src = mask_d[row:row + 1, :] if isinstance(t, int) else mask_d[bass.ds(row, 1), :]
                    sp.dma_start(mask[:, v, :, :].rearrange("p a c -> p (a c)"),
                                 src.to_broadcast([P, 2 * ATT])).then_inc(mask_landed[v], 16)
            steps(sp, step)

            for u in range(RING):
                sp.wait_ge(rows_stored[u], 16 * (TILES // RING))
            sp.wait_ge(recidx_ready, 1)
            sp.dma_start(recidx_d.unsqueeze(0), rec_idxrow[:, :]).then_inc(recidx_landed, 16)
            for a in range(2):
                sp.dma_start(sum_rows[0:TILES, a, :],
                             sums_d[NUM_ROWS + a * TILES:NUM_ROWS + (a + 1) * TILES, :]).then_inc(r_loaded, 16)
            sp.wait_ge(recidx_landed, 16)
            with nc.allow_non_contiguous_dma(reason="248 indices"):
                sp.dma_start(rec_idx[0:TILES, :], recidx_d.rearrange("(a t) -> t a", a=2)).then_inc(recidx_landed, 16)
            sp.dma_start(x_rows[0:125, :], x_d.rearrange("(p r) f -> p (r f)", p=125)).then_inc(x_landed, 16)
            sp.wait_ge(r_stored, 32)
            for c in range(5):
                if c >= 2:
                    sp.wait_ge(f_used, c - 1)
                sp.dma_start(em[:, c % 2, 0:5, :, :, :].rearrange("p s i m o -> p (s i m o)"),
                             sums_d[0:NUM_ROWS, :].rearrange("(p c r) k -> p c (r k)", p=P, c=5)[:, c, :]
                             ).then_inc(f_loaded[c % 2], 16)
            sp.wait_ge(f_out, 1)
            sp.dma_start(out_d.rearrange("(p r) f -> p (r f)", p=125), out_rows[0:125, :]).then_inc(out_stored, 16)
            sp.wait_ge(out_stored, 16)

        @block.gpsimd
        def _(pool):
            nc.gpsimd.iota(row_iota[:, :], [[1, P]], base=0, channel_multiplier=0,
                           allow_small_or_imprecise_dtypes=True).then_inc(iotas, 1)
            nc.gpsimd.iota(part_iota[:, :], [[0, 1]], base=0, channel_multiplier=1,
                           allow_small_or_imprecise_dtypes=True).then_inc(iotas, 1)
            nc.gpsimd.iota(node_iota[:, :], [[1, NODE_COLS + 1]], base=0, channel_multiplier=NODE_COLS,
                           allow_small_or_imprecise_dtypes=True).then_inc(iotas, 1)
            nc.gpsimd.iota(chunk_iota[:, :], [[1, P]], base=0, channel_multiplier=P,
                           allow_small_or_imprecise_dtypes=True).then_inc(iotas, 1)
            nc.gpsimd.iota(twice_tile[:, :], [[0, 1]], base=0, channel_multiplier=2,
                           allow_small_or_imprecise_dtypes=True).then_inc(iotas, 1)

            def gather(out, src, idx):
                return nc.gpsimd.indirect_dma_start(out, None, src, bass.IndirectOffsetOnAxis(idx, 0))

            pool.wait_ge(seg_ready, 1)
            for j in range(NODE_COLS + 1):
                gather(sub_last[:, j, :], sub_last_d, seg_i[:, j:j + 1]).then_inc(sub_landed, 16)
            pool.wait_ge(blk_ready, 1)
            for j in range(NODE_COLS + 1):
                gather(blk_dst[:, j, :], dst_d, blk_i[:, j:j + 1]).then_inc(dst_landed, 16)
            pool.wait_ge(entry_ready, 1)
            pool.wait_ge(zeroed, 48)
            for j in range(NODE_COLS):
                nc.gpsimd.indirect_dma_start(chunk_d, bass.IndirectOffsetOnAxis(chunk0_i[:, j:j + 1], 0),
                                             entry[:, j, :], None).then_inc(entry_stored, 16)

            last_row = pool.to_reg(NUM_ROWS + RECORDS - 1)

            def go():
                pool.sem_inc(pool_go, 1)

            def step(t, u):
                if valid(t, 4):
                    v = u % RING
                    since(pool, blk_idx_ready, t + 5)
                    since(pool, part1, t + 1)
                    since(pool, rest1, t + 1)
                    since(pool, x_idx_ready, t + 1)
                    since(pool, inv_ready, t + 1)
                    go()
                    gather(rec[:, v, :], rec_d, blk_idx[:, v:v + 1]).then_inc(rec_landed[v], 16)
                if valid(t, 3):
                    v = (u + 3) % RING
                    if isinstance(t, int) and t == -3:
                        pool.wait_ge(xpad_done, 32)
                    since(pool, x_idx_ready, t + 4)
                    since(pool, times_h, 4 * t)
                    go()
                    for s in range(SLOTS):
                        gather(h[:, v, s * FEAT:(s + 1) * FEAT], xpad_d, x_idx[:, v, s:s + 1]).then_inc(h_landed[v], 16)
                if valid(t, -3):
                    v = (u - 3) % RING
                    since(pool, sum_idx_ready, t - 2)
                    since(pool, sums_copied, t - 2)
                    go()
                    nc.gpsimd.indirect_dma_start(sums_d, bass.IndirectOffsetOnAxis(sum_idx[:, v:v + 1], 0),
                                                 sum_rows[:, v, :], None, bounds_check=last_row,
                                                 oob_is_err=False).then_inc(rows_stored[v], 16)
            steps(pool, step)
            pool.wait_ge(recidx_landed, 32)
            pool.wait_ge(r_rows, 2)
            for a in range(2):
                nc.gpsimd.indirect_dma_start(sums_d, bass.IndirectOffsetOnAxis(rec_idx[0:TILES, a:a + 1], 0),
                                             em[0:TILES, 2 + a, 0, :, :, :].rearrange("p i m o -> p (i m o)"), None,
                                             bounds_check=NUM_ROWS - 1, oob_is_err=False).then_inc(r_stored, 16)

        @block.scalar
        def _(act):
            def step(t, u):
                if valid(t, 4):
                    if isinstance(t, int) and t == FIRST - 1:
                        act.wait_ge(chunk_cols, 4)
                    col = t + 4
                    nc.scalar.copy(blk_idx[:, u:u + 1],
                                   t_blk[:, col:col + 1] if isinstance(t, int) else t_blk[:, bass.ds(col, 1)]
                                   ).then_inc(blk_idx_ready, 1)
                if valid(t, 3):
                    w, v = (u + 3) % 2, (u + 3) % RING
                    landed(act, rec_landed, t + 3, v)
                    since(act, t_ready, t + 2)
                    feats = rec[:, v, 0:SLOTS * FEAT].rearrange("p (s k) -> p s k", s=SLOTS)
                    nc.scalar.copy(parts[:, w, :, 0:48].rearrange("p s (d k) -> p s d k", d=3),
                                   bc(feats, 2, [P, SLOTS, 3, FEAT])).then_inc(part1, 1)
                if valid(t, 3):
                    act.wait_ge(rest1, t + 4)
                    w = (u + 3) % 2
                    nc.scalar.copy(parts[:, w, :, 48:80].rearrange("p s (d k) -> p s d k", d=2),
                                   bc(rest[:, w, :, :], 2, [P, SLOTS, 2, FEAT])).then_inc(part2, 1)
                if valid(t, 2):
                    w = u % 2
                    act.wait_ge(t_ready, t + 3)
                    since(act, prod_ready, 4 * (t + 1))
                    nc.scalar.copy(partsT[:, w, :], bank_t[0:KROWS, :]).then_inc(t_copied, 1)
                if valid(t, 0):
                    act.wait_ge(shifted, t + 1)
                    e = em[:, u, :, :, 0, :]
                    nc.scalar.activation(e, e, ACT.Exp).then_inc(exp_done, 1)
                if valid(t, 3):
                    act.wait_ge(rest2, t + 4)
                    w = (u + 3) % 2
                    nc.scalar.copy(parts[:, w, :, 80:96], rest[:, w, :, :]).then_inc(part3, 1)
                if valid(t, 1):
                    w = (u + 1) % 2
                    act.wait_ge(rev_done, t + 2)
                    dst = rec_max[:, :, t + 1, :] if isinstance(t, int) else rec_max[:, :, bass.ds(t + 1, 1), :].rearrange("p a t b -> p a (t b)")
                    nm = node_max[:, w, :].rearrange("p (a c) -> p a c", a=2)
                    nc.scalar.copy(dst, nm[:, :, 0:P:P - 1]).then_inc(rec_max_ready, 1)
                if valid(t, -2):
                    v = (u - 2) % RING
                    if not (isinstance(t, int) and t - 6 < 0):
                        landed(act, rows_stored, t - 6, v)
                    col = t - 2
                    nc.scalar.copy(sum_idx[:, v:v + 1],
                                   t_idx[:, col:col + 1] if isinstance(t, int) else t_idx[:, bass.ds(col, 1)]
                                   ).then_inc(sum_idx_ready, 1)
                    act.wait_ge(sums_ready, t - 1)
                    nc.scalar.copy(sum_rows[:, v, :], bank_sum[:, :]).then_inc(sums_copied, 1)
            steps(act, step)
            act.wait_ge(r_loaded, 32)
            for g in range(2):
                nc.scalar.copy(sum_rows[0:TILES, 2 + g, :].rearrange("p (m i o) -> p m i o", m=2, i=FEAT),
                               sum_rows[0:TILES, g, :].rearrange("p (i m o) -> p m i o", m=2, o=FEAT)
                               ).then_inc(r_grouped, 1)
            act.wait_ge(r_diff, 1)
            nc.scalar.activation(r_weight[:, :, :], r_shift[:, :, :], ACT.Exp).then_inc(r_exp, 1)
            act.wait_ge(f_var, 1)
            nc.scalar.activation(f_stat[:, 2, :], f_stat[:, 1, :], ACT.Sqrt, bias=eps[:, 0:1],
                                 scale=1.0 / FEAT).then_inc(f_std, 1)

        @block.tensor
        def _(pe):
            pe.wait_ge(total_ready, 1)
            nc.tensor.matmul(bank_max[:, 0:1], before[:, :], chunk_sum[:, NODE_COLS - 1:NODE_COLS],
                             start=True, stop=True).then_inc(carry_ps, 1)
            pe.wait_ge(last_ready, 1)
            nc.tensor.transpose(bank_max[0:2, 0:TILES], tile_carry[:, :], ident[0:TILES, 0:TILES]).then_inc(last_ps, 1)
            pe.wait_ge(last_ready, 2)
            nc.tensor.transpose(bank_max[0:TILES, 128:130], tile_last[:, 0:TILES], ident[0:2, 0:2]).then_inc(last_ps, 1)
            pe.wait_ge(chunk_ready, 1)
            for k, src in enumerate([c_node, c_blk, c_row, c_idx]):
                nc.tensor.transpose(bank_sum[:, k * P:k * P + TILES], src[:, :], ident[0:TILES, 0:TILES]).then_inc(chunk_ps, 1)
            pe.wait_ge(chunk_cols, 4)
            pe.wait_ge(w_placed, 160)

            def step(t, u):
                def sum_slots(slots):
                    if not valid(t, -2):
                        return
                    v = (u - 2) % RING
                    if slots[0] == 0:
                        pe.wait_ge(weighted, t - 1)
                        pe.wait_ge(onehot_ready, t - 1)
                        since(pe, sums_copied, t - 2)
                    for s in slots:
                        mm = nc.tensor.matmul(bank_sum[:, :], row_onehot[:, v, :],
                                              em[:, v, s, :, :, :].rearrange("p i m o -> p (i m o)"),
                                              start=(s == 0), stop=(s == SLOTS - 1))
                    if slots[-1] == SLOTS - 1:
                        mm.then_inc(sums_ready, 1)

                def transpose_parts():
                    if not valid(t, 2):
                        return
                    w = u % 2
                    pe.wait_ge(part3, t + 3)
                    pe.wait_ge(part2, t + 3)
                    pe.wait_ge(part1, t + 3)
                    pe.wait_ge(inv_ready, t + 3)
                    since(pe, t_copied, t + 2)
                    for s in range(SLOTS):
                        mm = nc.tensor.transpose(bank_t[0:KROWS, s * P:(s + 1) * P], parts[:, w, s, :], ident16[:, :])
                    mm.then_inc(t_ready, 1)

                for j in range(4):
                    if valid(t, 1):
                        w = (u + 1) % 2
                        if j == 0:
                            pe.wait_ge(t_copied, t + 2)
                        since(pe, times_h, 4 * (t + 1) + j - 1)
                        for s in range(2):
                            mm = nc.tensor.matmul(bank_prod[j % 2][:, s, :],
                                                  partsT[:, w, (2 * j + s) * P:(2 * j + s + 1) * P],
                                                  w_rows[:, :], start=True, stop=True)
                        mm.then_inc(prod_ready, 1)
                    if j == 1:
                        transpose_parts()
                    if j >= 1:
                        sum_slots([j - 1])
                sum_slots([3, 4, 5])
                if valid(t, 1):
                    w = (u + 1) % 2
                    pe.wait_ge(max_step, 3 * (t + 2))
                    since(pe, fwd_done, t + 1)
                    for a in range(2):
                        mm = nc.tensor.transpose(maxT_ps[:, a * P:(a + 1) * P],
                                                 chunk_max[:, w, a * P:(a + 1) * P], ident[:, :])
                    mm.then_inc(maxT_ready, 1)
                sum_slots([6, 7])
                if valid(t, 1):
                    w = (u + 1) % 2
                    pe.wait_ge(rev_done, t + 2)
                    since(pe, shifted, t + 1)
                    for a in range(2):
                        mm = nc.tensor.transpose(max_ps[:, a * P:(a + 1) * P],
                                                 node_max[:, w, a * P:(a + 1) * P], ident[:, :])
                    mm.then_inc(max_back, 1)
            steps(pe, step)

            pe.wait_ge(r_grouped, 2)
            for m in range(2):
                for a in range(2):
                    for g in range(2):
                        k = m * 2 + a
                        src = sum_rows[0:TILES, 2 + g, k * P:(k + 1) * P]
                        nc.tensor.transpose(bank_prod[m][:, a, g * TILES:(g + 1) * TILES], src,
                                            ident[0:TILES, 0:TILES]).then_inc(r_t, 1)
            pe.wait_ge(r_total, 1)
            for m in range(2):
                for a in range(2):
                    for g in range(2):
                        k = m * 2 + a
                        nc.tensor.transpose(bank_prod[g][0:TILES, 0, k * P:(k + 1) * P],
                                            r_acc[:, k, g * TILES:(g + 1) * TILES], ident[:, :]).then_inc(r_back, 1)

        @block.vector
        def _(v_eng):
            count = [0]

            def link(ins):
                count[0] += 1
                ins.then_inc(dve, 1)
                v_eng.wait_ge(dve, count[0])

            V = nc.vector
            v_eng.wait_ge(iotas, 5)
            link(V.memset(w_neg[:, :], 0.0))
            V.memset(ones[:, :], 1.0).then_inc(consts, 1)
            V.memset(zeros[:, :], 0.0).then_inc(consts, 1)
            v_eng.wait_ge(consts, 2)
            link(V.memset(eps[:, :], EPS))
            link(V.memset(parts[:, :, :, 96:100], 1.0))
            link(V.memset(w_neg[:, :].rearrange("p (i m o) -> p i m o", m=2, o=FEAT)[:, :, 0, :], NEG))
            link(V.tensor_scalar(before[:, :], row_iota[:, :], part_iota[:, 0:1], None, ALU.is_gt))
            link(V.tensor_scalar(ident[:, :], row_iota[:, :], part_iota[:, 0:1], None, ALU.is_equal))
            link(V.tensor_scalar(ident16[:, :], row_iota[:, :], part_iota[:, 0:1], None, ALU.is_equal))

            v_eng.wait_ge(loads, 48)
            C = NODE_COLS + 1

            def count_less(values, width, out):
                link(V.tensor_tensor(less[:, :, 0:width], values, bc(node_iota[:, :], 2, [P, C, width]), ALU.is_lt))
                link(V.tensor_reduce(out, less[:, :, 0:width], AX.X, ALU.add))

            count_less(bc(seg_last[:, :], 1, [P, C, 125]), 125, tmp[:, :])
            link(V.tensor_scalar(seg_f[:, :], tmp[:, :], 124.0, None, ALU.min))
            V.tensor_copy(seg_i[:, :], seg_f[:, :]).then_inc(seg_ready, 1)
            link(V.tensor_copy(w_part[:, 0, :], w_all[:, :]))
            link(V.tensor_tensor(w_rest[:, :], w_all[:, :], w_part[:, 0, :], ALU.subtract))
            link(V.tensor_copy(w_part[:, 1, :], w_rest[:, :]))
            link(V.tensor_tensor(w_rest[:, :], w_rest[:, :], w_part[:, 1, :], ALU.subtract))
            V.tensor_copy(w_part[:, 2, :], w_rest[:, :]).then_inc(w_split, 1)
            v_eng.wait_ge(sub_landed, 16 * C)
            count_less(sub_last[:, :, :], SUB, tmp[:, :])
            link(V.scalar_tensor_tensor(out=blk_f[:, :], in0=seg_f[:, :], scalar=float(SUB), in1=tmp[:, :],
                                        op0=ALU.mult, op1=ALU.add))
            link(V.tensor_scalar(blk_f[:, :], blk_f[:, :], float(NUM_BLOCKS - 1), None, ALU.min))
            V.tensor_copy(blk_i[:, :], blk_f[:, :]).then_inc(blk_ready, 1)
            v_eng.wait_ge(dst_landed, 16 * C)
            count_less(blk_dst[:, :, :], SLOTS, tmp[:, :])
            link(V.scalar_tensor_tensor(out=start[:, :], in0=blk_f[:, :], scalar=float(SLOTS), in1=tmp[:, :],
                                        op0=ALU.mult, op1=ALU.add))
            link(V.tensor_tensor(has_edges[:, :], start[:, 1:C], start[:, 0:NODE_COLS], ALU.is_gt))
            link(V.tensor_scalar(tmp[:, :], start[:, :], 1.0, 0.0, ALU.subtract, ALU.max))
            link(V.tensor_copy(start_i[:, :], start[:, :]))
            link(V.tensor_copy(last_i[:, :], tmp[:, :]))
            link(V.tensor_scalar(start_i[:, :], start_i[:, :], 3, None, ALU.arith_shift_right))
            link(V.tensor_scalar(last_i[:, :], last_i[:, :], 3, None, ALU.arith_shift_right))
            link(V.tensor_copy(blk0[:, :], start_i[:, :]))
            link(V.tensor_copy(blk1[:, :], last_i[:, :]))
            link(V.tensor_tensor(num_chunks[:, :], blk1[:, 1:C], blk0[:, 0:NODE_COLS], ALU.subtract))
            link(V.tensor_scalar(num_chunks[:, :], num_chunks[:, :], 1.0, 1.0, ALU.add, ALU.max))
            V.tensor_tensor_scan(chunk_sum[:, :], zeros[:, 0:NODE_COLS], num_chunks[:, :], 0.0,
                                 ALU.add, ALU.add).then_inc(total_ready, 1)
            v_eng.wait_ge(carry_ps, 1)
            link(V.tensor_copy(carry[:, :], bank_max[:, 0:1]))
            link(V.scalar_tensor_tensor(out=tmp[:, 0:NODE_COLS], in0=chunk_sum[:, :], scalar=carry[:, 0:1],
                                        in1=num_chunks[:, :], op0=ALU.add, op1=ALU.subtract))
            link(V.tensor_copy(chunk0_i[:, :], tmp[:, 0:NODE_COLS]))
            link(V.tensor_copy(entry[:, :, 0], node_iota[:, 0:NODE_COLS]))
            V.tensor_tensor(entry[:, :, 1], tmp[:, 0:NODE_COLS], blk0[:, 0:NODE_COLS],
                            ALU.subtract).then_inc(entry_ready, 1)

            v_eng.wait_ge(table_landed, 16)
            for a in range(2):
                link(V.tensor_tensor_scan(filled[:, a, :], zeros[0:TILES, 0:P], table[:, :, a], 0.0,
                                          ALU.add, ALU.max))
            link(V.memset(tile_last[:, :], 0.0))
            V.tensor_copy(tile_carry[:, :], filled[:, :, P - 1]).then_inc(last_ready, 1)
            v_eng.wait_ge(last_ps, 1)
            V.tensor_tensor_scan(tile_last[:, 1:TILES + 1], zeros[0:2, 0:TILES], bank_max[0:2, 0:TILES], 0.0,
                                 ALU.add, ALU.max).then_inc(last_ready, 1)
            v_eng.wait_ge(last_ps, 2)
            link(V.tensor_copy(tile_carry[:, :], bank_max[0:TILES, 128:130]))
            link(V.tensor_scalar(c_node[:, :], filled[:, 0, :], tile_carry[:, 0:1], None, ALU.max))
            link(V.tensor_scalar(c_a[:, :], filled[:, 1, :], tile_carry[:, 1:2], None, ALU.max))
            link(V.tensor_tensor(c_b[:, :], chunk_iota[:, :], c_a[:, :], ALU.subtract))
            link(V.tensor_scalar(c_blk[:, :], c_b[:, :], float(NUM_BLOCKS - 1), None, ALU.min))
            link(V.tensor_copy(c_ends[:, :], c_node[:, 0:P:P - 1]))
            link(V.tensor_scalar(c_row[:, :], c_node[:, :], c_ends[:, 0:1], None, ALU.subtract))
            link(V.memset(c_mask[:, :, :, :], CUT))
            link(V.tensor_tensor(c_a[:, 1:P], c_node[:, 1:P], c_node[:, 0:P - 1], ALU.not_equal))
            for b in range(2):
                link(V.tensor_scalar(c_mask[:, 0, b, 1:P], c_a[:, 1:P], CUT, None, ALU.mult))
                link(V.tensor_scalar(c_mask[:, 1, b, 0:P - 1], c_a[:, 1:P], CUT, None, ALU.mult))
            link(V.tensor_scalar(c_idx[:, :], row_iota[0:TILES, :], c_ends[:, 0:1], None, ALU.add))
            link(V.tensor_scalar(c_a[:, :], c_idx[:, :], c_ends[:, 1:2], SKIP, ALU.is_gt, ALU.mult))
            link(V.tensor_scalar(c_b[:, :], c_idx[:, :], c_ends[:, 1:2], None, ALU.is_equal))
            link(V.tensor_scalar(c_ext[:, 0:1], twice_tile[:, :], float(NUM_ROWS + 1), c_ends[:, 1:2], ALU.add, ALU.subtract))
            link(V.tensor_scalar(c_b[:, :], c_b[:, :], c_ext[:, 0:1], None, ALU.mult))
            link(V.tensor_tensor(c_idx[:, :], c_idx[:, :], c_b[:, :], ALU.add))
            link(V.tensor_tensor(c_idx[:, :], c_idx[:, :], c_a[:, :], ALU.add))
            V.tensor_scalar(c_idx[:, 0:1], twice_tile[:, :], float(NUM_ROWS), None, ALU.add).then_inc(chunk_ready, 1)
            for k, dst in enumerate([t_node, t_blk, t_row, t_idx]):
                v_eng.wait_ge(chunk_ps, 4)
                V.tensor_copy(dst[:, :], bank_sum[:, k * P:k * P + TILES]).then_inc(chunk_cols, 1)
            v_eng.wait_ge(chunk_cols, 4)

            def col(tab, t):
                return tab[:, t:t + 1] if isinstance(t, int) else tab[:, bass.ds(t, 1)]

            def step(t, u):
                if valid(t, 3):
                    v, w = (u + 3) % RING, (u + 3) % 2
                    landed(v_eng, rec_landed, t + 3, v)
                    src = rec[:, v, 128:136].bitcast(I32)
                    dst = rec[:, v, 136:144].bitcast(I32)
                    node = col(t_node, t + 3)
                    V.tensor_scalar(src1[:, w, :], src, 1.0, None, ALU.add).then_inc(src_step, 1)
                    since(v_eng, t_ready, t + 2)
                    V.tensor_scalar(parts[:, w, :, 99], dst, node, None, ALU.not_equal).then_inc(inv_ready, 1)
                    v_eng.wait_ge(src_step, t + 4)
                    V.scalar_tensor_tensor(out=x_idx[:, v, :], in0=dst, scalar=node, in1=src1[:, w, :],
                                           op0=ALU.is_equal, op1=ALU.mult).then_inc(x_idx_ready, 1)
                    v_eng.wait_ge(part1, t + 4)
                    feats = rec[:, v, 0:SLOTS * FEAT].rearrange("p (s k) -> p s k", s=SLOTS)
                    since(v_eng, part3, t + 2)
                    V.tensor_tensor(rest[:, w, :, :], feats, parts[:, w, :, 0:16], ALU.subtract).then_inc(rest1, 1)
                if valid(t, 1):
                    v, w = (u + 1) % RING, (u + 1) % 2
                    landed(v_eng, h_landed, t + 1, v, each=SLOTS)
                    since(v_eng, sums_ready, t - 2)
                    for j in range(4):
                        v_eng.wait_ge(prod_ready, 4 * (t + 1) + j + 1)
                        V.tensor_tensor(em[:, v, 2 * j:2 * j + 2, :, :, :].rearrange("p s i m o -> p (s i) (m o)"),
                                        bank_prod[j % 2][:, :, :].rearrange("p s (i x) -> p (s i) x", i=FEAT),
                                        bc(h[:, v, 32 * j:32 * j + 32], 2, [P, 32, 32]),
                                        ALU.mult).then_inc(times_h, 1)
                    v_eng.wait_ge(times_h, 4 * (t + 2))
                    V.tensor_tensor(max4[:, :, :, :], em[:, v, 0:4, :, 0, :], em[:, v, 4:8, :, 0, :],
                                    ALU.max).then_inc(max_step, 1)
                    v_eng.wait_ge(max_step, 3 * (t + 1) + 1)
                    V.tensor_tensor(max2[:, :, :, :], max4[:, 0:2, :, :], max4[:, 2:4, :, :], ALU.max).then_inc(max_step, 1)
                    v_eng.wait_ge(max_step, 3 * (t + 1) + 2)
                    since(v_eng, maxT_ready, t)
                    V.tensor_tensor(chunk_max[:, w, :].rearrange("p (i o) -> p i o", i=FEAT), max2[:, 0, :, :],
                                    max2[:, 1, :, :], ALU.max).then_inc(max_step, 1)
                if valid(t, 0):
                    v_eng.wait_ge(max_back, t + 1)
                    e = em[:, u, :, :, 0, :]
                    V.tensor_tensor(e, e, bc(max_ps.rearrange("p (i o) -> p i o", i=FEAT), 1, [P, SLOTS, FEAT, FEAT]),
                                    ALU.subtract).then_inc(shifted, 1)
                    V.tensor_scalar(row_onehot[:, u, :], row_iota[:, :], col(t_row, t), None,
                                    ALU.is_equal).then_inc(onehot_ready, 1)
                if valid(t, 3):
                    w = (u + 3) % 2
                    v_eng.wait_ge(part2, t + 4)
                    V.tensor_tensor(rest[:, w, :, :], rest[:, w, :, :], parts[:, w, :, 48:64], ALU.subtract).then_inc(rest2, 1)
                if valid(t, 1):
                    w = (u + 1) % 2
                    landed(v_eng, mask_landed, t + 1, w, size=2)
                    v_eng.wait_ge(maxT_ready, t + 2)
                    since(v_eng, rev_done, t + 1)
                    V.tensor_tensor_scan(fwd_max[:, :], mask[:, w, 0, :], maxT_ps, CUT, ALU.add,
                                         ALU.max).then_inc(fwd_done, 1)
                    v_eng.wait_ge(fwd_done, t + 2)
                    since(v_eng, max_back, t)
                    since(v_eng, rec_max_ready, t)
                    V.tensor_tensor_scan(node_max[:, w, ::-1], mask[:, w, 1, ::-1], fwd_max[:, ::-1], CUT, ALU.add,
                                         ALU.max).then_inc(rev_done, 1)
                if valid(t, -1):
                    v = (u - 1) % RING
                    v_eng.wait_ge(exp_done, t)
                    m = em[:, v, :, :, 1, :]
                    V.tensor_tensor(m, m, em[:, v, :, :, 0, :], ALU.mult).then_inc(weighted, 1)
            steps(v_eng, step)

            v_eng.wait_ge(recnode_landed, 16)
            v_eng.wait_ge(rec_max_ready, TILES)
            for k in range(3):
                link(V.memset(r_masks[:, k, :], CUT if k < 2 else 0.0))
            link(V.tensor_tensor(r_sum[:, 0, 1:RECORDS], rec_node[:, 1:RECORDS], rec_node[:, 0:RECORDS - 1], ALU.is_equal))
            same = r_sum[:, 0, 1:RECORDS]
            link(V.tensor_copy(r_masks[:, 2, 1:RECORDS], same))
            link(V.tensor_scalar(r_masks[:, 0, 1:RECORDS], same, 1.0, -CUT, ALU.subtract, ALU.mult))
            link(V.tensor_copy(r_masks[:, 1, 0:RECORDS - 1], r_masks[:, 0, 1:RECORDS]))
            link(V.tensor_scalar(r_sum[0:1, 1, 0:RECORDS - 1], r_sum[0:1, 0, 1:RECORDS], SKIP, None, ALU.mult))
            link(V.memset(r_sum[0:1, 1, RECORDS - 1:RECORDS], 0.0))
            V.tensor_tensor(rec_idxrow[:, :], r_sum[0:1, 1, :], rec_node[0:1, :], ALU.add).then_inc(recidx_ready, 1)
            for a in range(2):
                m = rec_max[:, a, :, :].rearrange("p t b -> p (t b)")
                link(V.tensor_tensor_scan(r_shift[:, a, :], r_masks[:, 0, :], m, CUT, ALU.add, ALU.max))
                link(V.tensor_tensor_scan(r_weight[:, a, ::-1], r_masks[:, 1, ::-1], r_shift[:, a, ::-1], CUT,
                                          ALU.add, ALU.max))
                link(V.tensor_tensor(r_shift[:, a, :], m, r_weight[:, a, :], ALU.subtract))
            V.tensor_copy(r_acc[:, 0, 0:1], r_shift[:, 0, 0:1]).then_inc(r_diff, 1)
            v_eng.wait_ge(r_exp, 1)
            v_eng.wait_ge(r_t, 8)
            for m in range(2):
                for a in range(2):
                    k = 2 * m + a
                    link(V.tensor_tensor(r_sum[:, k, :], bank_prod[m][:, a, 0:RECORDS], r_weight[:, a, :], ALU.mult))
                    last = V.tensor_tensor_scan(r_acc[:, k, :], r_masks[:, 2, :], r_sum[:, k, :], 0.0, ALU.mult, ALU.add)
                    if k < 3:
                        link(last)
            last.then_inc(r_total, 1)
            v_eng.wait_ge(r_back, 8)
            for g in range(2):
                V.tensor_copy(em[0:TILES, 2 + g, 0, :, :, :].rearrange("p i m o -> p m i o"),
                              bank_prod[g][0:TILES, 0, :].rearrange("p (m i o) -> p m i o", m=2, i=FEAT)
                              ).then_inc(r_rows, 1)

            for c in range(5):
                v_eng.wait_ge(f_loaded[c % 2], 16 * (c // 2 + 1))
                e = em[:, c % 2, 0:5, :, 0, :]
                m = em[:, c % 2, 0:5, :, 1, :]
                link(V.reciprocal(e, e))
                link(V.tensor_tensor(m, m, e, ALU.mult))
                V.tensor_reduce(f_sum[:, 5 * c:5 * c + 5, :], m.rearrange("p s i o -> p s o i"), AX.X,
                                ALU.add).then_inc(f_used, 1)
            v_eng.wait_ge(f_used, 5)
            link(V.tensor_tensor(f_sum[:, :, :], f_sum[:, :, :], bc(has_edges[:, :], 2, [P, NODE_COLS, FEAT]), ALU.mult))
            v_eng.wait_ge(x_landed, 16)
            flat = f_sum[0:125, :, :].rearrange("p j f -> p (j f)")
            link(V.tensor_tensor(flat, flat, x_rows[0:125, :], ALU.add))
            link(V.tensor_reduce(f_stat[:, 0, :], f_sum[:, :, :], AX.X, ALU.add))
            link(V.tensor_scalar(f_stat[:, 0, :], f_stat[:, 0, :], 1.0 / FEAT, None, ALU.mult))
            link(V.tensor_tensor(f_sum[:, :, :], f_sum[:, :, :], bc(f_stat[:, 0, :], 2, [P, NODE_COLS, FEAT]), ALU.subtract))
            link(V.tensor_tensor(f_mid[:, :, :], f_sum[:, :, :], f_sum[:, :, :], ALU.mult))
            V.tensor_reduce(f_stat[:, 1, :], f_mid[:, :, :], AX.X, ALU.add).then_inc(f_var, 1)
            v_eng.wait_ge(f_std, 1)
            link(V.reciprocal(f_stat[:, 3, :], f_stat[:, 2, :]))
            V.tensor_tensor(out_rows[:, :].rearrange("p (j f) -> p j f", f=FEAT), f_sum[:, :, :],
                            bc(f_stat[:, 3, :], 2, [P, NODE_COLS, FEAT]), ALU.mult).then_inc(f_out, 1)


def kernel(x, src, dst, edge_attr_16, L0_gnn_W_msg, L0_gnn_b_msg, L0_gnn_W_attn, L0_gnn_b_attn):
    import numpy as np
    import concourse.bacc as bacc
    from concourse.bass_utils import run_bass_kernel_spmd

    src, dst = np.asarray(src), np.asarray(dst)
    records = np.concatenate([np.asarray(edge_attr_16).reshape(NUM_BLOCKS, SLOTS * FEAT),
                              src.reshape(NUM_BLOCKS, SLOTS).view(np.float32),
                              dst.reshape(NUM_BLOCKS, SLOTS).view(np.float32)], axis=1)
    w = np.stack([np.asarray(L0_gnn_W_attn).reshape(FEAT, FEAT, FEAT),
                  np.asarray(L0_gnn_W_msg).reshape(FEAT, FEAT, FEAT)], axis=2).reshape(FEAT, BOTH)
    b = np.stack([np.asarray(L0_gnn_b_attn).reshape(FEAT, FEAT),
                  np.asarray(L0_gnn_b_msg).reshape(FEAT, FEAT)], axis=1).reshape(1, BOTH)
    arrays = {
        "records": records,
        "dst_blocks": dst.reshape(NUM_BLOCKS, SLOTS),
        "dst_sub_last": np.ascontiguousarray(dst[SLOTS - 1::SLOTS]).reshape(125, SUB),
        "dst_seg_last": np.ascontiguousarray(dst[SEG - 1::SEG]),
        "x": np.asarray(x),
        "w": w,
        "b": b,
    }
    nc = bacc.Bacc("TRN2", target_bir_lowering=False, num_devices=1)
    args = [nc.dram_tensor(f"in_{k}", a.shape, mybir.dt.from_np(a.dtype), kind="ExternalInput").ap()
            for k, a in arrays.items()]
    out = nc.dram_tensor("out_0", (NUM_NODES, FEAT), F32, kind="ExternalOutput").ap()
    gnn_kernel(nc, *args, out)
    r = run_bass_kernel_spmd(nc, [{f"in_{k}": a for k, a in arrays.items()}], core_ids=[0])
    return r.results[0]["out_0"]
```

```python
from contextlib import ExitStack

import concourse.bass as bass
from concourse import mybir

F32 = mybir.dt.float32
BF16 = mybir.dt.bfloat16
I32 = mybir.dt.int32
ALU = mybir.AluOpType
ACT = mybir.ActivationFunctionType
AX = mybir.AxisListType

P = 128
NUM_NODES = 3125
NUM_EDGES = 100000
FEAT = 16
SLOTS = 8
NUM_BLOCKS = NUM_EDGES // SLOTS
REC = SLOTS * FEAT + 2 * SLOTS
NODE_COLS = 25
NUM_ROWS = P * NODE_COLS
NUM_SEGS = 125
SEG = NUM_EDGES // NUM_SEGS
SUB = SEG // SLOTS
PREP_P = 100
PREP_GROUPS = 25
PREP_BLOCKS = NUM_BLOCKS // (PREP_P * PREP_GROUPS)
TILES = 4 * -(-(NUM_BLOCKS + NUM_ROWS) // (4 * P))
CHUNKS = TILES * P
RECORDS = 2 * TILES
ATT = FEAT * FEAT
BOTH = 2 * ATT
KROWS = 6 * FEAT + 4
NEG = -2.0 ** 99
CUT = -2.0 ** 101
SKIP = 60000.0
EPS = 1e-5
PARTS = SLOTS * KROWS
SPLIT = PARTS + 4 * SLOTS
RING = 4


def gnn_kernel(nc, rec_d, dst_d, sub_last_d, seg_last_d, x_d, w_d, b_d, out_d):
    xpad_d = nc.dram_tensor("xpad", [NUM_NODES + 1, FEAT], F32, kind="Internal").ap()
    chunk_d = nc.dram_tensor("chunk_table", [CHUNKS, 2], F32, kind="Internal").ap()
    split_d = nc.dram_tensor("split_records", [NUM_BLOCKS, SPLIT], BF16, kind="Internal").ap()
    recmax_d = nc.dram_tensor("record_maxima", [RECORDS, ATT], F32, kind="Internal").ap()
    mask_d = nc.dram_tensor("mask_table", [TILES, 3 * P], BF16, kind="Internal").ap()
    recnode_d = nc.dram_tensor("record_nodes", [RECORDS], F32, kind="Internal").ap()
    recidx_d = nc.dram_tensor("record_index", [RECORDS], I32, kind="Internal").ap()
    sums_d = nc.dram_tensor("sums", [NUM_ROWS + RECORDS, BOTH], F32, kind="Internal").ap()

    with ExitStack() as ctx:
        def sb(name, shape, dt=F32):
            return ctx.enter_context(nc.sbuf_tensor(name, shape, dt))

        def ps(name, shape, dt=F32):
            return ctx.enter_context(nc.psum_tensor(name, shape, dt))

        def sem(name):
            return ctx.enter_context(nc.semaphore(name))

        row_iota = sb("row_iota", [P, P])
        part_iota = sb("part_iota", [P, 1])
        node_iota = sb("node_iota", [P, NODE_COLS + 1])
        chunk_iota = sb("chunk_iota", [TILES, P])
        twice_tile = sb("twice_tile", [TILES, 1])
        ident = sb("ident", [P, P])
        ident16 = sb("ident16", [P, P], BF16)
        before = sb("before", [P, P])
        zeros = sb("zeros", [P, BOTH])
        ones = sb("ones", [1, FEAT])
        w_all = sb("w_all", [17, BOTH])
        w_rest = sb("w_rest", [17, BOTH])
        w_part = sb("w_part", [17, 3, BOTH], BF16)
        w_neg = sb("w_neg", [1, BOTH], BF16)
        w_rows = sb("w_rows", [KROWS, BOTH], BF16)
        seg_last = sb("seg_last", [P, NUM_SEGS], I32)
        seg_f = sb("seg_f", [P, NODE_COLS + 1])
        seg_i = sb("seg_i", [P, NODE_COLS + 1], I32)
        blk_f = sb("blk_f", [P, NODE_COLS + 1])
        blk_i = sb("blk_i", [P, NODE_COLS + 1], I32)
        start = sb("start", [P, NODE_COLS + 1])
        start_i = sb("start_i", [P, NODE_COLS + 1], I32)
        last_i = sb("last_i", [P, NODE_COLS + 1], I32)
        blk0 = sb("blk0", [P, NODE_COLS + 1])
        blk1 = sb("blk1", [P, NODE_COLS + 1])
        tmp = sb("tmp", [P, NODE_COLS + 1])
        num_chunks = sb("num_chunks", [P, NODE_COLS])
        chunk_sum = sb("chunk_sum", [P, NODE_COLS])
        carry = sb("carry", [P, 1])
        chunk0_i = sb("chunk0_i", [P, NODE_COLS], I32)
        entry = sb("entry", [P, NODE_COLS, 2])
        has_edges = sb("has_edges", [P, NODE_COLS])
        table = sb("table", [TILES, P, 2])
        filled = sb("filled", [TILES, 2, P])
        tile_last = sb("tile_last", [2, TILES + 1])
        tile_carry = sb("tile_carry", [TILES, 2])
        c_node = sb("c_node", [TILES, P])
        c_blk = sb("c_blk", [TILES, P])
        c_row = sb("c_row", [TILES, P])
        c_idx = sb("c_idx", [TILES, P])
        c_a = sb("c_a", [TILES, P])
        c_b = sb("c_b", [TILES, P])
        c_ends = sb("c_ends", [TILES, 2])
        c_ext = sb("c_ext", [TILES, 1])
        c_mask = sb("c_mask", [TILES, 3, P], BF16)
        t_node = sb("t_node", [P, TILES])
        t_blk = sb("t_blk", [P, TILES])
        t_negrow = sb("t_negrow", [P, TILES])
        t_idx = sb("t_idx", [P, TILES])
        blk_idx = sb("blk_idx", [P, RING], I32)
        rec = sb("rec", [P, RING, SPLIT], BF16)
        src1 = sb("src1", [P, 2, SLOTS])
        x_idx = sb("x_idx", [P, RING, SLOTS], I32)
        h = sb("h", [P, RING, SLOTS * FEAT])
        partsT = sb("partsT", [KROWS, 2, SLOTS * P], BF16)
        em = sb("em", [P, RING, SLOTS, FEAT, 2, FEAT])
        max4 = sb("max4", [P, 4, FEAT, FEAT])
        max2 = sb("max2", [P, 2, FEAT, FEAT])
        chunk_max = sb("chunk_max", [P, 2, ATT])
        mask = sb("mask", [P, 2, 3 * P], BF16)
        fwd_max = sb("fwd_max", [P, ATT])
        chunk_fwd = sb("chunk_fwd", [P, ATT])
        last_onehot = sb("last_onehot", [P, 2, P])
        off_diag = sb("off_diag", [P, P])
        node_max = sb("node_max", [P, 2, ATT])
        row_onehot = sb("row_onehot", [P, RING, P])
        off_row = sb("off_row", [P, P])
        minus_part = sb("minus_part", [P, 1])
        one_col = sb("one_col", [P, 1])
        in_rec = sb("in_rec", [PREP_P, 5, PREP_BLOCKS, REC])
        in_rest = sb("in_rest", [PREP_P, 5, PREP_BLOCKS, SLOTS, FEAT])
        split = sb("split", [PREP_P, 5, PREP_BLOCKS, SPLIT], BF16)
        sum_rows = sb("sum_rows", [P, RING, BOTH])
        sum_idx = sb("sum_idx", [P, RING], I32)
        rec_max = sb("rec_max", [TILES, 2, ATT])
        rec_node = sb("rec_node", [P, RECORDS])
        rec_idx = sb("rec_idx", [P, 2], I32)
        rec_idxrow = sb("rec_idxrow", [1, RECORDS], I32)
        r_masks = sb("r_masks", [P, 3, RECORDS])
        r_weight = sb("r_weight", [P, 2, RECORDS])
        x_rows = sb("x_rows", [P, NODE_COLS * FEAT])
        out_rows = sb("out_rows", [P, NODE_COLS * FEAT])
        f_sum = sb("f_sum", [P, NODE_COLS, FEAT])
        f_stat = sb("f_stat", [P, 4, NODE_COLS])
        eps = sb("eps", [P, 1])

        bank_prod = [ps(f"bank_prod{i}", [P, 2, BOTH]) for i in range(2)]
        bank_t = ps("bank_t", [P, SLOTS * P], BF16)
        bank_max = ps("bank_max", [P, BOTH])
        bank_maxT = ps("bank_maxT", [P, BOTH])
        bank_sum = ps("bank_sum", [P, BOTH])
        maxT_ps = bank_maxT[:, 0:ATT]
        max_ps = bank_max[:, 0:ATT]

        em_flat = em[:, :, :, :, :, :].rearrange("p r s i m o -> p (r s i m o)")
        cols = NODE_COLS + 1
        sub_last = em_flat[:, 0:cols * SUB].bitcast(I32).rearrange("p (c e) -> p c e", c=cols)
        blk_dst = em_flat[:, cols * SUB:cols * (SUB + SLOTS)].bitcast(I32).rearrange("p (c e) -> p c e", c=cols)
        less = em_flat[:, cols * (SUB + SLOTS):cols * (SUB + SLOTS + NUM_SEGS)].rearrange("p (c e) -> p c e", c=cols)

        def view(base, k):
            return em_flat[:, base:base + k * RECORDS].rearrange("p (k r) -> p k r", k=k)

        half_tile = RING * SLOTS * BOTH // 8
        r_sum, r_acc = view(5 * half_tile, 4), view(5 * half_tile + 4 * RECORDS, 4)

        r_shift = view(7 * half_tile, 2)
        f_mid = em_flat[:, 8 * half_tile - NODE_COLS * FEAT:8 * half_tile].rearrange("p (j f) -> p j f", f=FEAT)

        iotas = sem("iotas")
        dve = sem("dve_step")
        loads = sem("loads")
        xpad_done = sem("xpad_done")
        zeroed = sem("zeroed")
        seg_ready = sem("seg_ready")
        sub_landed = sem("sub_landed")
        blk_ready = sem("blk_ready")
        dst_landed = sem("dst_landed")
        in_landed = [sem(f"in_landed{u}") for u in range(5)]
        in_part1 = sem("in_part1")
        in_rest1 = sem("in_rest1")
        in_part2 = sem("in_part2")
        in_rest2 = sem("in_rest2")
        in_part3 = sem("in_part3")
        in_copies = sem("in_copies")
        in_copied = sem("in_copied")
        split_stored = [sem(f"split_stored{u}") for u in range(5)]
        consts = sem("consts")
        total_ready = sem("total_ready")
        carry_ps = sem("carry_ps")
        entry_ready = sem("entry_ready")
        entry_stored = sem("entry_stored")
        table_landed = sem("table_landed")
        last_ready = sem("last_ready")
        last_ps = sem("last_ps")
        chunk_ready = sem("chunk_ready")
        chunk_ps = sem("chunk_ps")
        chunk_cols = sem("chunk_cols")
        masks_stored = sem("masks_stored")
        recnode_landed = sem("recnode_landed")
        recidx_ready = sem("recidx_ready")
        recidx_landed = sem("recidx_landed")
        w_split = sem("w_split")
        w_placed = sem("w_placed")

        blk_idx_ready = sem("blk_idx_ready")
        rec_landed = [sem(f"rec_landed{u}") for u in range(RING)]
        src_step = sem("src_step")
        x_idx_ready = sem("x_idx_ready")
        h_landed = [sem(f"h_landed{u}") for u in range(RING)]
        inv_ready = sem("inv_ready")
        t_ready = sem("t_ready")
        t_copied = sem("t_copied")
        prod_ready = sem("prod_ready")
        times_h = sem("times_h")
        max_step = sem("max_step")
        maxT_ready = sem("maxT_ready")
        fwd_done = sem("fwd_done")
        fwd_back = sem("fwd_back")
        fwd_copied = sem("fwd_copied")
        last_off = sem("last_off")
        last_ready_t = sem("last_ready_t")
        row_off = sem("row_off")
        max_copied = sem("max_copied")
        recmax_stored = [sem(f"recmax_stored{u}") for u in range(2)]
        max_back = sem("max_back")
        shifted = sem("shifted")
        exp_done = sem("exp_done")
        weighted = sem("weighted")
        last_weighted = sem("last_weighted")
        onehot_ready = sem("onehot_ready")
        sums_ready = sem("sums_ready")
        sums_copied = sem("sums_copied")
        sum_idx_ready = sem("sum_idx_ready")
        rows_stored = [sem(f"rows_stored{u}") for u in range(RING)]
        mask_landed = [sem(f"mask_landed{u}") for u in range(2)]

        r_loaded = sem("r_loaded")
        sp_go = sem("sp_go")
        pool_go = sem("pool_go")
        recmax_landed = sem("recmax_landed")
        recmax_ps = sem("recmax_ps")
        r_grouped = sem("r_grouped")
        r_t = sem("r_t")
        r_diff = sem("r_diff")
        r_exp = sem("r_exp")
        r_total = sem("r_total")
        r_back = sem("r_back")
        r_rows = sem("r_rows")
        r_stored = sem("r_stored")
        f_loaded = [sem(f"f_loaded{u}") for u in range(2)]
        f_used = sem("f_used")
        x_landed = sem("x_landed")
        f_var = sem("f_var")
        f_std = sem("f_std")
        f_out = sem("f_out")
        out_stored = sem("out_stored")

        block = ctx.enter_context(nc.Block())

        def bc(ap, axis, shape):
            return ap.unsqueeze(axis).to_broadcast(shape)

        FIRST, LAST = -3, TILES + 2
        STEADY = (8, TILES - 4)

        def steps(eng, body):
            for t in range(FIRST - 1, STEADY[0]):
                body(t, t % RING)
            with eng.Fori(STEADY[0], STEADY[1] - RING + 1, RING) as t0:
                for u in range(RING):
                    body(t0 + u, u)
            for t in range(STEADY[1], LAST + 1):
                body(t, t % RING)

        def valid(t, shift):
            return not isinstance(t, int) or 0 <= t + shift < TILES

        def since(eng, s, count):
            if not isinstance(count, int) or count > 0:
                eng.wait_ge(s, count)

        def landed(eng, ring, t, u, each=1, size=RING):
            if isinstance(t, int):
                since(eng, ring[u], 16 * each * (t // size + 1))
            else:
                eng.wait_ge(ring[u], (t - u) * (16 * each // size) + 16 * each)

        @block.sync
        def _(sp):
            def go():
                sp.sem_inc(sp_go, 1)

            in_v = rec_d.rearrange("(p g b) w -> p g (b w)", p=PREP_P, g=PREP_GROUPS)

            def load_records(g, u):
                src = in_v[:, g, :] if isinstance(g, int) else in_v[:, bass.ds(g, 1), :].rearrange("p g w -> p (g w)")
                sp.dma_start(in_rec[:, u, :, :].rearrange("p b w -> p (b w)"), src).then_inc(in_landed[u], 16)

            sp.dma_start(seg_last[:, :], seg_last_d.partition_broadcast(P)).then_inc(loads, 16)
            sp.dma_start(w_all[0:16, :], w_d).then_inc(loads, 16)
            sp.dma_start(w_all[16:17, :], b_d).then_inc(loads, 16)
            sp.dma_start(xpad_d[1:NUM_NODES + 1, :], x_d).then_inc(xpad_done, 16)
            for u in range(5):
                load_records(u, u)
            sp.wait_ge(consts, 2)
            sp.dma_start(xpad_d[0:1, :], ones[:, :]).then_inc(xpad_done, 16)
            sp.dma_start(chunk_d.rearrange("(t j) c -> t (j c)", t=TILES), zeros[0:TILES, 0:2 * P]).then_inc(zeroed, 16)
            for a in range(2):
                sp.dma_start(sums_d[NUM_ROWS + a * TILES:NUM_ROWS + (a + 1) * TILES, :],
                             zeros[0:TILES, :]).then_inc(zeroed, 16)
            sp.wait_ge(w_split, 1)
            for k, part in enumerate([0, 1, 2, 0, 1, 0]):
                sp.dma_start(w_rows[16 * k:16 * k + 16, :], w_part[0:16, part, :]).then_inc(w_placed, 16)
            for part in range(3):
                sp.dma_start(w_rows[96 + part:97 + part, :], w_part[16:17, part, :]).then_inc(w_placed, 16)
            sp.dma_start(w_rows[99:100, :], w_neg[:, :]).then_inc(w_placed, 16)

            out_v = split_d.rearrange("(p g b) w -> p g (b w)", p=PREP_P, g=PREP_GROUPS)

            def store_split(g, u):
                sp.wait_ge(in_part3, g + 1)
                go()
                sp.wait_ge(in_copies, 3 * (g + 1))
                go()
                sp.wait_ge(in_copied, g + 1)
                go()
                dst = out_v[:, g, :] if isinstance(g, int) else out_v[:, bass.ds(g, 1), :].rearrange("p g w -> p (g w)")
                sp.dma_start(dst, split[:, u, :, :].rearrange("p b w -> p (b w)")).then_inc(split_stored[u], 16)
            for u in range(5):
                store_split(u, u)
                load_records(u + 5, u)
            with sp.Fori(5, PREP_GROUPS - 9, 5) as g0:
                for u in range(5):
                    store_split(g0 + u, u)
                    load_records(g0 + u + 5, u)
            for u in range(5):
                store_split(PREP_GROUPS - 5 + u, u)
            sp.wait_ge(entry_stored, 16 * NODE_COLS)
            sp.dma_start(table[:, :, :], chunk_d.rearrange("(t j) c -> t j c", t=TILES)).then_inc(table_landed, 16)
            sp.wait_ge(chunk_ready, 1)
            sp.dma_start(mask_d, c_mask[:, :, :].rearrange("t a j -> t (a j)")).then_inc(masks_stored, 16)
            sp.dma_start(recnode_d.rearrange("(t a) -> t a", a=2), c_ends[:, :]).then_inc(masks_stored, 16)
            sp.wait_ge(masks_stored, 32)
            sp.dma_start(rec_node[:, :], recnode_d.partition_broadcast(P)).then_inc(recnode_landed, 16)

            def step(t, u):
                if valid(t, 2):
                    since(sp, fwd_done, t + 1)
                    go()
                    since(sp, last_off, t + 1)
                    go()
                    v = u % 2
                    row = t + 2
                    src = mask_d[row:row + 1, :] if isinstance(t, int) else mask_d[bass.ds(row, 1), :]
                    sp.dma_start(mask[:, v, :], src.to_broadcast([P, 3 * P])).then_inc(mask_landed[v], 16)
                if valid(t, 0):
                    sp.wait_ge(max_copied, t + 1)
                    go()
                    for e in range(2):
                        row = 2 * t + e
                        dst = recmax_d[row:row + 1, :] if isinstance(t, int) else recmax_d[bass.ds(row, 1), :]
                        part = e * (P - 1)
                        sp.dma_start(dst, node_max[part:part + 1, u % 2, :]).then_inc(recmax_stored[u % 2], 16)
            steps(sp, step)

            sp.wait_ge(recidx_ready, 1)
            sp.dma_start(recidx_d.unsqueeze(0), rec_idxrow[:, :]).then_inc(recidx_landed, 16)
            sp.dma_start(x_rows[0:125, :], x_d.rearrange("(p r) f -> p (r f)", p=125)).then_inc(x_landed, 16)
            for u in range(2):
                sp.wait_ge(recmax_stored[u], 16 * TILES)
            for a in range(2):
                sp.dma_start(rec_max[:, a, :], recmax_d[a * TILES:(a + 1) * TILES, :]).then_inc(recmax_landed, 16)
            for u in range(RING):
                sp.wait_ge(rows_stored[u], 16 * (TILES // RING))
            for a in range(2):
                sp.dma_start(sum_rows[0:TILES, a, :],
                             sums_d[NUM_ROWS + a * TILES:NUM_ROWS + (a + 1) * TILES, :]).then_inc(r_loaded, 16)
            sp.wait_ge(recidx_landed, 16)
            with nc.allow_non_contiguous_dma(reason="248 indices"):
                sp.dma_start(rec_idx[0:TILES, :], recidx_d.rearrange("(a t) -> t a", a=2)).then_inc(recidx_landed, 16)
            sp.wait_ge(r_stored, 32)
            for c in range(5):
                if c >= 2:
                    sp.wait_ge(f_used, c - 1)
                sp.dma_start(em[:, c % 2, 0:5, :, :, :].rearrange("p s i m o -> p (s i m o)"),
                             sums_d[0:NUM_ROWS, :].rearrange("(p c r) k -> p c (r k)", p=P, c=5)[:, c, :]
                             ).then_inc(f_loaded[c % 2], 16)
            sp.wait_ge(f_out, 1)
            sp.dma_start(out_d.rearrange("(p r) f -> p (r f)", p=125), out_rows[0:125, :]).then_inc(out_stored, 16)
            sp.wait_ge(out_stored, 16)

        @block.gpsimd
        def _(pool):
            nc.gpsimd.iota(row_iota[:, :], [[1, P]], base=0, channel_multiplier=0,
                           allow_small_or_imprecise_dtypes=True).then_inc(iotas, 1)
            nc.gpsimd.iota(part_iota[:, :], [[0, 1]], base=0, channel_multiplier=1,
                           allow_small_or_imprecise_dtypes=True).then_inc(iotas, 1)
            nc.gpsimd.iota(node_iota[:, :], [[1, NODE_COLS + 1]], base=0, channel_multiplier=NODE_COLS,
                           allow_small_or_imprecise_dtypes=True).then_inc(iotas, 1)
            nc.gpsimd.iota(chunk_iota[:, :], [[1, P]], base=0, channel_multiplier=P,
                           allow_small_or_imprecise_dtypes=True).then_inc(iotas, 1)
            nc.gpsimd.iota(twice_tile[:, :], [[0, 1]], base=0, channel_multiplier=2,
                           allow_small_or_imprecise_dtypes=True).then_inc(iotas, 1)

            def gather(out, src, idx):
                return nc.gpsimd.indirect_dma_start(out, None, src, bass.IndirectOffsetOnAxis(idx, 0))

            pool.wait_ge(seg_ready, 1)
            for j in range(cols):
                gather(sub_last[:, j, :], sub_last_d, seg_i[:, j:j + 1]).then_inc(sub_landed, 16)
            pool.wait_ge(blk_ready, 1)
            for j in range(cols):
                gather(blk_dst[:, j, :], dst_d, blk_i[:, j:j + 1]).then_inc(dst_landed, 16)
            pool.wait_ge(entry_ready, 1)
            pool.wait_ge(zeroed, 48)
            for j in range(NODE_COLS):
                nc.gpsimd.indirect_dma_start(chunk_d, bass.IndirectOffsetOnAxis(chunk0_i[:, j:j + 1], 0),
                                             entry[:, j, :], None).then_inc(entry_stored, 16)

            last_row = pool.to_reg(NUM_ROWS + RECORDS - 1)

            def go():
                pool.sem_inc(pool_go, 1)

            def step(t, u):
                if valid(t, 4):
                    v = u % RING
                    since(pool, blk_idx_ready, t + 5)
                    since(pool, t_ready, t + 1)
                    since(pool, x_idx_ready, t + 1)
                    if isinstance(t, int) and t == FIRST - 1:
                        for g in range(5):
                            pool.wait_ge(split_stored[g], 16 * PREP_GROUPS // 5)
                    go()
                    gather(rec[:, v, :], split_d, blk_idx[:, v:v + 1]).then_inc(rec_landed[v], 16)
                def gather_features(slots):
                    v = (u + 3) % RING
                    for s in slots:
                        gather(h[:, v, s * FEAT:(s + 1) * FEAT], xpad_d, x_idx[:, v, s:s + 1]).then_inc(h_landed[v], 16)

                if valid(t, 3):
                    if isinstance(t, int) and t == -3:
                        pool.wait_ge(xpad_done, 32)
                    since(pool, x_idx_ready, t + 4)
                    since(pool, times_h, 4 * t)
                    go()
                    gather_features(range(4))
                if valid(t, -1):
                    v = (u - 1) % RING
                    pool.wait_ge(exp_done, t)
                    nc.gpsimd.tensor_tensor(em[:, v, SLOTS - 1, :, 1, :], em[:, v, SLOTS - 1, :, 1, :],
                                            em[:, v, SLOTS - 1, :, 0, :], ALU.mult).then_inc(last_weighted, 1)
                if valid(t, 3):
                    gather_features(range(4, SLOTS))
                if valid(t, -3):
                    v = (u - 3) % RING
                    since(pool, sum_idx_ready, t - 2)
                    since(pool, sums_copied, t - 2)
                    go()
                    nc.gpsimd.indirect_dma_start(sums_d, bass.IndirectOffsetOnAxis(sum_idx[:, v:v + 1], 0),
                                                 sum_rows[:, v, :], None, bounds_check=last_row,
                                                 oob_is_err=False).then_inc(rows_stored[v], 16)
            steps(pool, step)
            pool.wait_ge(recidx_landed, 32)
            pool.wait_ge(r_rows, 2)
            for a in range(2):
                nc.gpsimd.indirect_dma_start(sums_d, bass.IndirectOffsetOnAxis(rec_idx[0:TILES, a:a + 1], 0),
                                             em[0:TILES, 2 + a, 0, :, :, :].rearrange("p i m o -> p (i m o)"), None,
                                             bounds_check=NUM_ROWS - 1, oob_is_err=False).then_inc(r_stored, 16)

        @block.scalar
        def _(act):
            act.wait_ge(consts, 2)

            def split_place(u):
                return split[:, u, :, 0:PARTS].rearrange("p b (s k) -> p b s k", s=SLOTS)

            def split_parts(g, u):
                if not isinstance(g, int) or g < PREP_GROUPS:
                    feats = in_rec[:, u, :, 0:SLOTS * FEAT]
                    if isinstance(g, int):
                        act.wait_ge(in_landed[u], 16)
                        if g == 0:
                            act.wait_ge(consts, 4)
                    else:
                        act.wait_ge(in_landed[u], (g - u) * 16 // 5 + 16)
                        act.wait_ge(split_stored[u], (g - u) * 16 // 5)
                    nc.scalar.copy(split_place(u)[:, :, :, 0:16],
                                   feats.rearrange("p b (s k) -> p b s k", s=SLOTS)).then_inc(in_part1, 1)
                if not isinstance(g, int) or 1 <= g <= PREP_GROUPS:
                    w = (u - 1) % 5
                    act.wait_ge(in_rest1, g)
                    nc.scalar.copy(split_place(w)[:, :, :, 48:64], in_rest[:, w, :, :, :]).then_inc(in_part2, 1)
                if not isinstance(g, int) or 2 <= g:
                    w = (u - 2) % 5
                    act.wait_ge(in_rest2, g - 1)
                    nc.scalar.copy(split_place(w)[:, :, :, 80:96], in_rest[:, w, :, :, :]).then_inc(in_part3, 1)

            for g in range(5):
                split_parts(g, g)
            with act.Fori(5, PREP_GROUPS - 4, 5) as g0:
                for u in range(5):
                    split_parts(g0 + u, u)
            for g in range(PREP_GROUPS, PREP_GROUPS + 2):
                split_parts(g, g % 5)

            def step(t, u):
                if valid(t, 4):
                    if isinstance(t, int) and t == FIRST - 1:
                        act.wait_ge(chunk_cols, 4)
                    col = t + 4
                    nc.scalar.copy(blk_idx[:, u:u + 1],
                                   t_blk[:, col:col + 1] if isinstance(t, int) else t_blk[:, bass.ds(col, 1)]
                                   ).then_inc(blk_idx_ready, 1)
                if valid(t, -1):
                    act.wait_ge(shifted, t)
                    e = em[:, (u - 1) % RING, :, :, 0, :]
                    nc.scalar.activation(e, e, ACT.Exp).then_inc(exp_done, 1)
                if valid(t, 2):
                    w = u % 2
                    act.wait_ge(t_ready, t + 3)
                    since(act, prod_ready, 4 * (t + 1))
                    nc.scalar.copy(partsT[:, w, :], bank_t[0:KROWS, :]).then_inc(t_copied, 1)
                if valid(t, 0):
                    act.wait_ge(fwd_back, t + 1)
                    since(act, max_back, t)
                    nc.scalar.copy(chunk_fwd[:, :], bank_maxT[:, ATT:BOTH]).then_inc(fwd_copied, 1)
                if valid(t, 0):
                    since(act, sums_ready, t - 3)
                    since(act, onehot_ready, t)
                    col = t_negrow[:, t:t + 1] if isinstance(t, int) else t_negrow[:, bass.ds(t, 1)]
                    nc.scalar.activation(off_row[:, :], row_iota[:, :], ACT.Abs, bias=col).then_inc(row_off, 1)
                    act.wait_ge(row_off, t + 1)
                    nc.scalar.activation(row_onehot[:, u, :], off_row[:, :], ACT.Relu, bias=one_col[:, 0:1],
                                         scale=-1.0).then_inc(onehot_ready, 1)
                if valid(t, 0):
                    act.wait_ge(max_back, t + 1)
                    if not (isinstance(t, int) and t < 2):
                        landed(act, recmax_stored, t - 2, u % 2, each=2, size=2)
                        act.wait_ge(shifted, t - 1)
                    nc.scalar.copy(node_max[:, u % 2, :], bank_max[:, 0:ATT]).then_inc(max_copied, 1)
                if valid(t, 1):
                    w = (u + 1) % 2
                    landed(act, mask_landed, t + 1, w, size=2)
                    since(act, last_ready_t, t + 1)
                    nc.scalar.activation(off_diag[:, :], mask[:, w, 2 * P:3 * P], ACT.Abs,
                                         bias=minus_part[:, 0:1]).then_inc(last_off, 1)
                    act.wait_ge(last_off, t + 2)
                    since(act, max_back, t)
                    nc.scalar.activation(last_onehot[:, w, :], off_diag[:, :], ACT.Relu, bias=one_col[:, 0:1],
                                         scale=-1.0).then_inc(last_ready_t, 1)
                if valid(t, -2):
                    v = (u - 2) % RING
                    if not (isinstance(t, int) and t - 6 < 0):
                        landed(act, rows_stored, t - 6, v)
                    col = t - 2
                    nc.scalar.copy(sum_idx[:, v:v + 1],
                                   t_idx[:, col:col + 1] if isinstance(t, int) else t_idx[:, bass.ds(col, 1)]
                                   ).then_inc(sum_idx_ready, 1)
                if valid(t, -2):
                    v = (u - 2) % RING
                    act.wait_ge(sums_ready, t - 1)
                    nc.scalar.copy(sum_rows[:, v, :], bank_sum[:, :]).then_inc(sums_copied, 1)
            steps(act, step)
            act.wait_ge(r_loaded, 32)
            for g in range(2):
                nc.scalar.copy(sum_rows[0:TILES, 2 + g, :].rearrange("p (m i o) -> p m i o", m=2, i=FEAT),
                               sum_rows[0:TILES, g, :].rearrange("p (i m o) -> p m i o", m=2, o=FEAT)
                               ).then_inc(r_grouped, 1)
            act.wait_ge(r_diff, 1)
            nc.scalar.activation(r_weight[:, :, :], r_shift[:, :, :], ACT.Exp).then_inc(r_exp, 1)
            act.wait_ge(f_var, 1)
            nc.scalar.activation(f_stat[:, 2, :], f_stat[:, 1, :], ACT.Sqrt, bias=eps[:, 0:1],
                                 scale=1.0 / FEAT).then_inc(f_std, 1)

        @block.tensor
        def _(pe):
            pe.wait_ge(total_ready, 1)
            nc.tensor.matmul(bank_max[:, 0:1], before[:, :], chunk_sum[:, NODE_COLS - 1:NODE_COLS],
                             start=True, stop=True).then_inc(carry_ps, 1)
            pe.wait_ge(last_ready, 1)
            nc.tensor.transpose(bank_max[0:2, 0:TILES], tile_carry[:, :], ident[0:TILES, 0:TILES]).then_inc(last_ps, 1)
            pe.wait_ge(last_ready, 2)
            nc.tensor.transpose(bank_max[0:TILES, 128:130], tile_last[:, 0:TILES], ident[0:2, 0:2]).then_inc(last_ps, 1)
            pe.wait_ge(chunk_ready, 1)
            for k, src in enumerate([c_node, c_blk, c_row, c_idx]):
                nc.tensor.transpose(bank_sum[:, k * P:k * P + TILES], src[:, :], ident[0:TILES, 0:TILES]).then_inc(chunk_ps, 1)
            pe.wait_ge(chunk_cols, 4)
            pe.wait_ge(w_placed, 160)

            def step(t, u):
                def sum_slots(slots):
                    if not valid(t, -2):
                        return
                    v = (u - 2) % RING
                    if slots[0] == 0:
                        pe.wait_ge(weighted, 2 * (t - 1))
                        pe.wait_ge(onehot_ready, t - 1)
                        since(pe, sums_copied, t - 2)
                    if slots[-1] == SLOTS - 1:
                        pe.wait_ge(last_weighted, t - 1)
                    for s in slots:
                        mm = nc.tensor.matmul(bank_sum[:, :], row_onehot[:, v, :],
                                              em[:, v, s, :, :, :].rearrange("p i m o -> p (i m o)"),
                                              start=(s == 0), stop=(s == SLOTS - 1))
                    if slots[-1] == SLOTS - 1:
                        mm.then_inc(sums_ready, 1)

                def transpose_parts():
                    if not valid(t, 2):
                        return
                    w = u % 2
                    v = (u + 2) % RING
                    pe.wait_ge(inv_ready, t + 3)
                    since(pe, t_copied, t + 2)
                    for s in range(SLOTS):
                        mm = nc.tensor.transpose(bank_t[0:KROWS, s * P:(s + 1) * P], rec[:, v, s * KROWS:(s + 1) * KROWS], ident16[:, :])
                    mm.then_inc(t_ready, 1)

                for j in range(4):
                    if valid(t, 1):
                        w = (u + 1) % 2
                        if j == 0:
                            pe.wait_ge(t_copied, t + 2)
                        since(pe, times_h, 4 * (t + 1) + j - 1)
                        for s in range(2):
                            mm = nc.tensor.matmul(bank_prod[j % 2][:, s, :],
                                                  partsT[:, w, (2 * j + s) * P:(2 * j + s + 1) * P],
                                                  w_rows[:, :], start=True, stop=True)
                        mm.then_inc(prod_ready, 1)
                    if j == 1:
                        if valid(t, 0):
                            pe.wait_ge(max_step, 3 * (t + 1))
                            since(pe, fwd_copied, t)
                            for a in range(2):
                                mm = nc.tensor.transpose(maxT_ps[:, a * P:(a + 1) * P],
                                                         chunk_max[:, u % 2, a * P:(a + 1) * P], ident[:, :])
                            mm.then_inc(maxT_ready, 1)
                        transpose_parts()
                        sum_slots([0])
                    if j == 2:
                        sum_slots([1])
                        if valid(t, 0):
                            pe.wait_ge(fwd_done, t + 1)
                            for a in range(2):
                                mm = nc.tensor.transpose(bank_maxT[:, ATT + a * P:ATT + (a + 1) * P],
                                                         fwd_max[:, a * P:(a + 1) * P], ident[:, :])
                            mm.then_inc(fwd_back, 1)
                    if j == 3:
                        sum_slots([2])
                        if valid(t, 0):
                            pe.wait_ge(fwd_copied, t + 1)
                            pe.wait_ge(last_ready_t, t + 1)
                            since(pe, max_copied, t)
                            nc.tensor.matmul(max_ps, last_onehot[:, u % 2, :], chunk_fwd[:, :],
                                             start=True, stop=True).then_inc(max_back, 1)
                sum_slots([3, 4, 5, 6, 7])
            steps(pe, step)

            pe.wait_ge(recmax_landed, 32)
            for a in range(2):
                for g in range(2):
                    nc.tensor.transpose(bank_maxT[:, a * RECORDS + g * TILES:a * RECORDS + (g + 1) * TILES],
                                        rec_max[:, g, a * P:(a + 1) * P], ident[0:TILES, 0:TILES]).then_inc(recmax_ps, 1)
            pe.wait_ge(r_grouped, 2)
            for m in range(2):
                for a in range(2):
                    for g in range(2):
                        k = m * 2 + a
                        src = sum_rows[0:TILES, 2 + g, k * P:(k + 1) * P]
                        nc.tensor.transpose(bank_prod[m][:, a, g * TILES:(g + 1) * TILES], src,
                                            ident[0:TILES, 0:TILES]).then_inc(r_t, 1)
            pe.wait_ge(r_total, 1)
            for m in range(2):
                for a in range(2):
                    for g in range(2):
                        k = m * 2 + a
                        nc.tensor.transpose(bank_prod[g][0:TILES, 0, k * P:(k + 1) * P],
                                            r_acc[:, k, g * TILES:(g + 1) * TILES], ident[:, :]).then_inc(r_back, 1)

        @block.vector
        def _(v_eng):
            count = [0]

            def link(ins):
                count[0] += 1
                ins.then_inc(dve, 1)
                v_eng.wait_ge(dve, count[0])

            V = nc.vector
            v_eng.wait_ge(iotas, 5)
            link(V.memset(w_neg[:, :], 0.0))
            V.memset(ones[:, :], 1.0).then_inc(consts, 1)
            V.memset(zeros[:, :], 0.0).then_inc(consts, 1)
            v_eng.wait_ge(consts, 2)
            link(V.memset(eps[:, :], EPS))
            for u in range(5):
                link(V.memset(split[:, u, :, 0:PARTS].rearrange("p b (s k) -> p b s k", s=SLOTS)[:, :, :, 96:100],
                              1.0))
            link(V.memset(one_col[:, :], 1.0))
            V.tensor_scalar(minus_part[:, :], part_iota[:, :], -1.0, None, ALU.mult).then_inc(consts, 2)
            link(V.memset(w_neg[:, :].rearrange("p (i m o) -> p i m o", m=2, o=FEAT)[:, :, 0, :], NEG))
            link(V.tensor_scalar(before[:, :], row_iota[:, :], part_iota[:, 0:1], None, ALU.is_gt))
            link(V.tensor_scalar(ident[:, :], row_iota[:, :], part_iota[:, 0:1], None, ALU.is_equal))
            link(V.tensor_scalar(ident16[:, :], row_iota[:, :], part_iota[:, 0:1], None, ALU.is_equal))

            v_eng.wait_ge(loads, 48)
            C = NODE_COLS + 1

            def count_less(values, width):
                link(V.tensor_tensor(less[:, :, 0:width], values, bc(node_iota[:, :], 2, [P, C, width]), ALU.is_lt))
                link(V.tensor_reduce(tmp[:, :], less[:, :, 0:width], AX.X, ALU.add))

            count_less(bc(seg_last[:, :], 1, [P, C, NUM_SEGS]), NUM_SEGS)
            link(V.tensor_scalar(seg_f[:, :], tmp[:, :], float(NUM_SEGS - 1), None, ALU.min))
            V.tensor_copy(seg_i[:, :], seg_f[:, :]).then_inc(seg_ready, 1)

            def split_rest(g, u):
                if not isinstance(g, int) or g < PREP_GROUPS:
                    place = split[:, u, :, 0:PARTS].rearrange("p b (s k) -> p b s k", s=SLOTS)
                    ints = split[:, u, :, PARTS:SPLIT].bitcast(I32)
                    feats = in_rec[:, u, :, 0:SLOTS * FEAT].rearrange("p b (s k) -> p b s k", s=SLOTS)
                    v_eng.wait_ge(in_part1, g + 1)
                    V.tensor_tensor(in_rest[:, u, :, :, :], feats, place[:, :, :, 0:16], ALU.subtract).then_inc(in_rest1, 1)
                    for k in (16, 32):
                        V.tensor_copy(place[:, :, :, k:k + 16], place[:, :, :, 0:16]).then_inc(in_copies, 1)
                    V.tensor_copy(ints, in_rec[:, u, :, SLOTS * FEAT:REC].bitcast(I32)).then_inc(in_copies, 1)
                if not isinstance(g, int) or g >= 1:
                    w = (u - 1) % 5
                    place = split[:, w, :, 0:PARTS].rearrange("p b (s k) -> p b s k", s=SLOTS)
                    rest = in_rest[:, w, :, :, :]
                    v_eng.wait_ge(in_part2, g)
                    V.tensor_tensor(rest, rest, place[:, :, :, 48:64], ALU.subtract).then_inc(in_rest2, 1)
                    V.tensor_copy(place[:, :, :, 64:80], place[:, :, :, 48:64]).then_inc(in_copied, 1)

            link(V.tensor_copy(w_part[:, 0, :], w_all[:, :]))
            link(V.tensor_tensor(w_rest[:, :], w_all[:, :], w_part[:, 0, :], ALU.subtract))
            link(V.tensor_copy(w_part[:, 1, :], w_rest[:, :]))
            link(V.tensor_tensor(w_rest[:, :], w_rest[:, :], w_part[:, 1, :], ALU.subtract))
            V.tensor_copy(w_part[:, 2, :], w_rest[:, :]).then_inc(w_split, 1)
            for u in range(5):
                split_rest(u, u)
            v_eng.wait_ge(sub_landed, 16 * C)
            count_less(sub_last, SUB)
            link(V.scalar_tensor_tensor(out=blk_f[:, :], in0=seg_f[:, :], scalar=float(SUB), in1=tmp[:, :],
                                        op0=ALU.mult, op1=ALU.add))
            link(V.tensor_scalar(blk_f[:, :], blk_f[:, :], float(NUM_BLOCKS - 1), None, ALU.min))
            V.tensor_copy(blk_i[:, :], blk_f[:, :]).then_inc(blk_ready, 1)
            with v_eng.Fori(5, 15 - 4, 5) as g0:
                for u in range(5):
                    split_rest(g0 + u, u)
            v_eng.wait_ge(dst_landed, 16 * C)
            count_less(blk_dst, SLOTS)
            link(V.scalar_tensor_tensor(out=start[:, :], in0=blk_f[:, :], scalar=float(SLOTS), in1=tmp[:, :],
                                        op0=ALU.mult, op1=ALU.add))
            link(V.tensor_tensor(has_edges[:, :], start[:, 1:C], start[:, 0:NODE_COLS], ALU.is_gt))
            link(V.tensor_scalar(tmp[:, :], start[:, :], 1.0, 0.0, ALU.subtract, ALU.max))
            link(V.tensor_copy(start_i[:, :], start[:, :]))
            link(V.tensor_copy(last_i[:, :], tmp[:, :]))
            link(V.tensor_scalar(start_i[:, :], start_i[:, :], 3, None, ALU.arith_shift_right))
            link(V.tensor_scalar(last_i[:, :], last_i[:, :], 3, None, ALU.arith_shift_right))
            link(V.tensor_copy(blk0[:, :], start_i[:, :]))
            link(V.tensor_copy(blk1[:, :], last_i[:, :]))
            link(V.tensor_tensor(num_chunks[:, :], blk1[:, 1:C], blk0[:, 0:NODE_COLS], ALU.subtract))
            link(V.tensor_scalar(num_chunks[:, :], num_chunks[:, :], 1.0, 1.0, ALU.add, ALU.max))
            V.tensor_tensor_scan(chunk_sum[:, :], zeros[:, 0:NODE_COLS], num_chunks[:, :], 0.0,
                                 ALU.add, ALU.add).then_inc(total_ready, 1)
            v_eng.wait_ge(carry_ps, 1)
            link(V.tensor_copy(carry[:, :], bank_max[:, 0:1]))
            link(V.scalar_tensor_tensor(out=tmp[:, 0:NODE_COLS], in0=chunk_sum[:, :], scalar=carry[:, 0:1],
                                        in1=num_chunks[:, :], op0=ALU.add, op1=ALU.subtract))
            link(V.tensor_copy(chunk0_i[:, :], tmp[:, 0:NODE_COLS]))
            link(V.tensor_copy(entry[:, :, 0], node_iota[:, 0:NODE_COLS]))
            V.tensor_tensor(entry[:, :, 1], tmp[:, 0:NODE_COLS], blk0[:, 0:NODE_COLS],
                            ALU.subtract).then_inc(entry_ready, 1)

            with v_eng.Fori(15, PREP_GROUPS - 4, 5) as g0:
                for u in range(5):
                    split_rest(g0 + u, u)
            split_rest(PREP_GROUPS, 0)

            v_eng.wait_ge(table_landed, 16)
            for a in range(2):
                link(V.tensor_tensor_scan(filled[:, a, :], zeros[0:TILES, 0:P], table[:, :, a], 0.0,
                                          ALU.add, ALU.max))
            link(V.memset(tile_last[:, :], 0.0))
            V.tensor_copy(tile_carry[:, :], filled[:, :, P - 1]).then_inc(last_ready, 1)
            v_eng.wait_ge(last_ps, 1)
            V.tensor_tensor_scan(tile_last[:, 1:TILES + 1], zeros[0:2, 0:TILES], bank_max[0:2, 0:TILES], 0.0,
                                 ALU.add, ALU.max).then_inc(last_ready, 1)
            v_eng.wait_ge(last_ps, 2)
            link(V.tensor_copy(tile_carry[:, :], bank_max[0:TILES, 128:130]))
            link(V.tensor_scalar(c_node[:, :], filled[:, 0, :], tile_carry[:, 0:1], None, ALU.max))
            link(V.tensor_scalar(c_a[:, :], filled[:, 1, :], tile_carry[:, 1:2], None, ALU.max))
            link(V.tensor_tensor(c_b[:, :], chunk_iota[:, :], c_a[:, :], ALU.subtract))
            link(V.tensor_scalar(c_blk[:, :], c_b[:, :], float(NUM_BLOCKS - 1), None, ALU.min))
            link(V.tensor_copy(c_ends[:, :], c_node[:, 0:P:P - 1]))
            link(V.tensor_scalar(c_row[:, :], c_node[:, :], c_ends[:, 0:1], -1.0, ALU.subtract, ALU.mult))
            link(V.memset(c_mask[:, :, :], CUT))
            link(V.tensor_tensor(c_a[:, 1:P], c_node[:, 1:P], c_node[:, 0:P - 1], ALU.not_equal))
            for b in range(2):
                link(V.tensor_scalar(c_mask[:, b, 1:P], c_a[:, 1:P], CUT, None, ALU.mult))
            link(V.memset(c_b[:, P - 1:P], float(P - 1)))
            link(V.tensor_scalar(c_b[:, 0:P - 1], c_a[:, 1:P], 1.0, -float(P), ALU.subtract, ALU.mult))
            link(V.tensor_tensor(c_b[:, 0:P - 1], c_b[:, 0:P - 1], row_iota[0:TILES, 0:P - 1], ALU.add))
            link(V.tensor_tensor_scan(c_a[:, ::-1], zeros[0:TILES, 0:P], c_b[:, ::-1], float(P), ALU.add, ALU.min))
            link(V.tensor_copy(c_mask[:, 2, :], c_a[:, :]))
            link(V.tensor_scalar(c_idx[:, :], row_iota[0:TILES, :], c_ends[:, 0:1], None, ALU.add))
            link(V.tensor_scalar(c_a[:, :], c_idx[:, :], c_ends[:, 1:2], SKIP, ALU.is_gt, ALU.mult))
            link(V.tensor_scalar(c_b[:, :], c_idx[:, :], c_ends[:, 1:2], None, ALU.is_equal))
            link(V.tensor_scalar(c_ext[:, 0:1], twice_tile[:, :], float(NUM_ROWS + 1), c_ends[:, 1:2], ALU.add, ALU.subtract))
            link(V.tensor_scalar(c_b[:, :], c_b[:, :], c_ext[:, 0:1], None, ALU.mult))
            link(V.tensor_tensor(c_idx[:, :], c_idx[:, :], c_b[:, :], ALU.add))
            link(V.tensor_tensor(c_idx[:, :], c_idx[:, :], c_a[:, :], ALU.add))
            V.tensor_scalar(c_idx[:, 0:1], twice_tile[:, :], float(NUM_ROWS), None, ALU.add).then_inc(chunk_ready, 1)
            for k, dst in enumerate([t_node, t_blk, t_negrow, t_idx]):
                v_eng.wait_ge(chunk_ps, 4)
                V.tensor_copy(dst[:, :], bank_sum[:, k * P:k * P + TILES]).then_inc(chunk_cols, 1)
            v_eng.wait_ge(chunk_cols, 4)

            def col(tab, t):
                return tab[:, t:t + 1] if isinstance(t, int) else tab[:, bass.ds(t, 1)]

            def step(t, u):
                if valid(t, 3):
                    v, w = (u + 3) % RING, (u + 3) % 2
                    landed(v_eng, rec_landed, t + 3, v)
                    src = rec[:, v, PARTS:PARTS + 2 * SLOTS].bitcast(I32)
                    dst = rec[:, v, PARTS + 2 * SLOTS:SPLIT].bitcast(I32)
                    node = col(t_node, t + 3)
                    V.tensor_scalar(src1[:, w, :], src, 1.0, None, ALU.add).then_inc(src_step, 1)
                    V.tensor_scalar(rec[:, v, KROWS - 1:PARTS:KROWS], dst, node, None,
                                    ALU.not_equal).then_inc(inv_ready, 1)
                    v_eng.wait_ge(src_step, t + 4)
                    V.scalar_tensor_tensor(out=x_idx[:, v, :], in0=dst, scalar=node, in1=src1[:, w, :],
                                           op0=ALU.is_equal, op1=ALU.mult).then_inc(x_idx_ready, 1)
                def times_features(pairs):
                    if not valid(t, 1):
                        return
                    v = (u + 1) % RING
                    if pairs[0] == 0:
                        landed(v_eng, h_landed, t + 1, v, each=SLOTS)
                        since(v_eng, sums_ready, t - 2)
                    for j in pairs:
                        v_eng.wait_ge(prod_ready, 4 * (t + 1) + j + 1)
                        V.tensor_tensor(em[:, v, 2 * j:2 * j + 2, :, :, :].rearrange("p s i m o -> p (s i) (m o)"),
                                        bank_prod[j % 2][:, :, :].rearrange("p s (i x) -> p (s i) x", i=FEAT),
                                        bc(h[:, v, 32 * j:32 * j + 32], 2, [P, 32, 32]),
                                        ALU.mult).then_inc(times_h, 1)

                def weigh(lo, hi):
                    if not valid(t, -1):
                        return
                    v = (u - 1) % RING
                    v_eng.wait_ge(exp_done, t)
                    m = em[:, v, lo:hi, :, 1, :]
                    V.tensor_tensor(m, m, em[:, v, lo:hi, :, 0, :], ALU.mult).then_inc(weighted, 1)

                times_features([0, 1])
                if valid(t, 0):
                    landed(v_eng, mask_landed, t, u % 2, size=2)
                    v_eng.wait_ge(maxT_ready, t + 1)
                    since(v_eng, fwd_back, t)
                    V.tensor_tensor_scan(fwd_max[:, :], mask[:, u % 2, 0:ATT], maxT_ps, CUT, ALU.add,
                                         ALU.max).then_inc(fwd_done, 1)
                times_features([2, 3])
                weigh(0, 4)
                if valid(t, 1):
                    v = (u + 1) % RING
                    v_eng.wait_ge(times_h, 4 * (t + 2))
                    V.tensor_tensor(max4[:, :, :, :], em[:, v, 0:4, :, 0, :], em[:, v, 4:8, :, 0, :],
                                    ALU.max).then_inc(max_step, 1)
                weigh(4, SLOTS - 1)
                if valid(t, 1):
                    v_eng.wait_ge(max_step, 3 * (t + 1) + 1)
                    V.tensor_tensor(max2[:, :, :, :], max4[:, 0:2, :, :], max4[:, 2:4, :, :], ALU.max).then_inc(max_step, 1)
                if valid(t, 0):
                    v_eng.wait_ge(max_copied, t + 1)
                    e = em[:, u, :, :, 0, :]
                    V.tensor_tensor(e, e, bc(node_max[:, u % 2, :].rearrange("p (i o) -> p i o", i=FEAT), 1,
                                             [P, SLOTS, FEAT, FEAT]), ALU.subtract).then_inc(shifted, 1)
                if valid(t, 1):
                    w = (u + 1) % 2
                    v_eng.wait_ge(max_step, 3 * (t + 1) + 2)
                    since(v_eng, maxT_ready, t)
                    V.tensor_tensor(chunk_max[:, w, :].rearrange("p (i o) -> p i o", i=FEAT), max2[:, 0, :, :],
                                    max2[:, 1, :, :], ALU.max).then_inc(max_step, 1)
            steps(v_eng, step)

            v_eng.wait_ge(recnode_landed, 16)
            for k in range(3):
                link(V.memset(r_masks[:, k, :], CUT if k < 2 else 0.0))
            link(V.tensor_tensor(r_weight[:, 0, 1:RECORDS], rec_node[:, 1:RECORDS], rec_node[:, 0:RECORDS - 1], ALU.is_equal))
            same = r_weight[:, 0, 1:RECORDS]
            link(V.tensor_copy(r_masks[:, 2, 1:RECORDS], same))
            link(V.tensor_scalar(r_masks[:, 0, 1:RECORDS], same, 1.0, -CUT, ALU.subtract, ALU.mult))
            link(V.tensor_copy(r_masks[:, 1, 0:RECORDS - 1], r_masks[:, 0, 1:RECORDS]))
            link(V.tensor_scalar(r_weight[0:1, 1, 0:RECORDS - 1], r_weight[0:1, 0, 1:RECORDS], SKIP, None, ALU.mult))
            link(V.memset(r_weight[0:1, 1, RECORDS - 1:RECORDS], 0.0))
            V.tensor_tensor(rec_idxrow[:, :], r_weight[0:1, 1, :], rec_node[0:1, :], ALU.add).then_inc(recidx_ready, 1)
            v_eng.wait_ge(recidx_ready, 1)
            v_eng.wait_ge(recmax_ps, 4)
            for a in range(2):
                m = bank_maxT[:, a * RECORDS:(a + 1) * RECORDS]
                link(V.tensor_tensor_scan(r_shift[:, a, :], r_masks[:, 0, :], m, CUT, ALU.add, ALU.max))
                link(V.tensor_tensor_scan(r_weight[:, a, ::-1], r_masks[:, 1, ::-1], r_shift[:, a, ::-1], CUT,
                                          ALU.add, ALU.max))
                link(V.tensor_tensor(r_shift[:, a, :], m, r_weight[:, a, :], ALU.subtract))
            V.tensor_copy(r_acc[:, 0, 0:1], r_shift[:, 0, 0:1]).then_inc(r_diff, 1)
            v_eng.wait_ge(r_exp, 1)
            v_eng.wait_ge(r_t, 8)
            for m in range(2):
                for a in range(2):
                    k = 2 * m + a
                    link(V.tensor_tensor(r_sum[:, k, :], bank_prod[m][:, a, 0:RECORDS], r_weight[:, a, :], ALU.mult))
                    last = V.tensor_tensor_scan(r_acc[:, k, :], r_masks[:, 2, :], r_sum[:, k, :], 0.0, ALU.mult, ALU.add)
                    if k < 3:
                        link(last)
            last.then_inc(r_total, 1)
            v_eng.wait_ge(r_back, 8)
            for g in range(2):
                V.tensor_copy(em[0:TILES, 2 + g, 0, :, :, :].rearrange("p i m o -> p m i o"),
                              bank_prod[g][0:TILES, 0, :].rearrange("p (m i o) -> p m i o", m=2, i=FEAT)
                              ).then_inc(r_rows, 1)

            for c in range(5):
                v_eng.wait_ge(f_loaded[c % 2], 16 * (c // 2 + 1))
                e = em[:, c % 2, 0:5, :, 0, :]
                m = em[:, c % 2, 0:5, :, 1, :]
                link(V.reciprocal(e, e))
                link(V.tensor_tensor(m, m, e, ALU.mult))
                V.tensor_reduce(f_sum[:, 5 * c:5 * c + 5, :], m.rearrange("p s i o -> p s o i"), AX.X,
                                ALU.add).then_inc(f_used, 1)
            v_eng.wait_ge(f_used, 5)
            link(V.tensor_tensor(f_sum[:, :, :], f_sum[:, :, :], bc(has_edges[:, :], 2, [P, NODE_COLS, FEAT]), ALU.mult))
            v_eng.wait_ge(x_landed, 16)
            flat = f_sum[0:125, :, :].rearrange("p j f -> p (j f)")
            link(V.tensor_tensor(flat, flat, x_rows[0:125, :], ALU.add))
            link(V.tensor_reduce(f_stat[:, 0, :], f_sum[:, :, :], AX.X, ALU.add))
            link(V.tensor_scalar(f_stat[:, 0, :], f_stat[:, 0, :], 1.0 / FEAT, None, ALU.mult))
            link(V.tensor_tensor(f_sum[:, :, :], f_sum[:, :, :], bc(f_stat[:, 0, :], 2, [P, NODE_COLS, FEAT]), ALU.subtract))
            link(V.tensor_tensor(f_mid[:, :, :], f_sum[:, :, :], f_sum[:, :, :], ALU.mult))
            V.tensor_reduce(f_stat[:, 1, :], f_mid[:, :, :], AX.X, ALU.add).then_inc(f_var, 1)
            v_eng.wait_ge(f_std, 1)
            link(V.reciprocal(f_stat[:, 3, :], f_stat[:, 2, :]))
            V.tensor_tensor(out_rows[:, :].rearrange("p (j f) -> p j f", f=FEAT), f_sum[:, :, :],
                            bc(f_stat[:, 3, :], 2, [P, NODE_COLS, FEAT]), ALU.mult).then_inc(f_out, 1)


def kernel(x, src, dst, edge_attr_16, L0_gnn_W_msg, L0_gnn_b_msg, L0_gnn_W_attn, L0_gnn_b_attn):
    import numpy as np
    import concourse.bacc as bacc
    from concourse.bass_utils import run_bass_kernel_spmd

    src, dst = np.asarray(src), np.asarray(dst)
    records = np.concatenate([np.asarray(edge_attr_16).reshape(NUM_BLOCKS, SLOTS * FEAT),
                              src.reshape(NUM_BLOCKS, SLOTS).view(np.float32),
                              dst.reshape(NUM_BLOCKS, SLOTS).view(np.float32)], axis=1)
    w = np.stack([np.asarray(L0_gnn_W_attn).reshape(FEAT, FEAT, FEAT),
                  np.asarray(L0_gnn_W_msg).reshape(FEAT, FEAT, FEAT)], axis=2).reshape(FEAT, BOTH)
    b = np.stack([np.asarray(L0_gnn_b_attn).reshape(FEAT, FEAT),
                  np.asarray(L0_gnn_b_msg).reshape(FEAT, FEAT)], axis=1).reshape(1, BOTH)
    arrays = {
        "records": records,
        "dst_blocks": dst.reshape(NUM_BLOCKS, SLOTS),
        "dst_sub_last": np.ascontiguousarray(dst[SLOTS - 1::SLOTS]).reshape(NUM_SEGS, SUB),
        "dst_seg_last": np.ascontiguousarray(dst[SEG - 1::SEG]),
        "x": np.asarray(x),
        "w": w,
        "b": b,
    }
    nc = bacc.Bacc("TRN2", target_bir_lowering=False, num_devices=1)
    args = [nc.dram_tensor(f"in_{k}", a.shape, mybir.dt.from_np(a.dtype), kind="ExternalInput").ap()
            for k, a in arrays.items()]
    out = nc.dram_tensor("out_0", (NUM_NODES, FEAT), F32, kind="ExternalOutput").ap()
    gnn_kernel(nc, *args, out)
    r = run_bass_kernel_spmd(nc, [{f"in_{k}": a for k, a in arrays.items()}], core_ids=[0])
    return r.results[0]["out_0"]
```
